# Optimizing a Trainium2 kernel written in Bass

```python
import numpy as np
import jax
import jax.numpy as jnp

def _softmax(x, axis=-1):
    return jax.nn.softmax(x, axis=axis)

def _gelu(x):
    return jax.nn.gelu(x, approximate=True)

def _silu(x):
    return jax.nn.silu(x)

def _sigmoid(x):
    return jax.nn.sigmoid(x)

def _layernorm(x, axis=-1, eps=1e-05):
    m = jnp.mean(x, axis=axis, keepdims=True)
    v = jnp.var(x, axis=axis, keepdims=True)
    return (x - m) / jnp.sqrt(v + eps)

def _scatter_add(tgt, idx, src, axis=0):
    return tgt.at[idx].add(src)

def _segment_sum(src, seg, n):
    return jax.ops.segment_sum(src, seg, n)
kernel_name = 'mk_lm_tower_d1_tok_ids1024_r4_ac1e2d'

def setup_inputs(seed: int=0):
    np.random.seed(seed)
    _w = jnp.asarray

    def _rec_inputs():
        import jax
        import jax.numpy as jnp
        _rk = jax.random.key(seed)
        x = jax.random.randint(jax.random.fold_in(_rk, 1), (32, 512), 0, 12564, jnp.int32)
        return x
    x = _rec_inputs()

    def _L0_tok_setup():
        import jax, jax.numpy as jnp
        import numpy as np
        VOCAB = 50257
        DIM = 256
        R = 16
        ALPHA = 32
        SCALING = ALPHA / R
        key = jax.random.key(seed)
        k1, k2, k3, k4 = jax.random.split(key, 4)
        input_ids = jax.random.randint(k1, (4, 1024), 0, VOCAB)
        emb_weight = jax.random.normal(k2, (VOCAB, DIM), dtype=jnp.float32)
        lora_A = jax.random.normal(k3, (R, VOCAB), dtype=jnp.float32) * (1.0 / R)
        lora_B = jax.random.normal(k4, (DIM, R), dtype=jnp.float32) * 0.02
        return {'input': input_ids, 'emb_weight': emb_weight, 'lora_A': lora_A, 'lora_B': lora_B}
    _L0_tok_all = _L0_tok_setup()
    _L0_tok_in = {k: v for k, v in _L0_tok_all.items() if k in ('emb_weight', 'lora_A', 'lora_B')}
    del _L0_tok_all

    def _L0_attn_setup():
        import jax, jax.numpy as jnp
        import numpy as np
        B, T, D, H = (1, 1024, 256, 16)
        HD = D // H
        W_LOCAL = 64
        N_GLOBAL = 64
        key = jax.random.key(seed)
        ks = jax.random.split(key, 7)
        s = 0.02
        return {'hidden_states': jax.random.normal(ks[0], (B, T, D), dtype=jnp.float32), 'Wqkv': jax.random.normal(ks[1], (D, 3 * D), dtype=jnp.float32) * s, 'bqkv': jnp.zeros((3 * D,), dtype=jnp.float32), 'Wout': jax.random.normal(ks[2], (D, D), dtype=jnp.float32) * s, 'bout': jnp.zeros((D,), dtype=jnp.float32), 'Wg': jax.random.normal(ks[3], (D, 1), dtype=jnp.float32) * s, 'bg': jnp.zeros((1,), dtype=jnp.float32)}
    _L0_attn_all = _L0_attn_setup()
    _L0_attn_in = {k: v for k, v in _L0_attn_all.items() if k in ('Wqkv', 'bqkv', 'Wout', 'bout', 'Wg', 'bg')}
    del _L0_attn_all

    def _L0_ffn_setup():
        import jax, jax.numpy as jnp
        import numpy as np
        NUM_EXPERTS = 8
        TOP_K = 2
        CAP_RATIO = 1.25
        INIT_STD = 0.02
        key = jax.random.key(seed)
        k1, k2, k3, k4 = jax.random.split(key, 4)
        B, T, H, F = (4, 512, 256, 1024)
        x = jax.random.normal(k1, (B, T, H), jnp.float32)
        router_w = jax.random.normal(k2, (NUM_EXPERTS, H), jnp.float32) * INIT_STD
        w1 = jax.random.normal(k3, (NUM_EXPERTS, H, F), jnp.float32) * INIT_STD
        w2 = jax.random.normal(k4, (NUM_EXPERTS, F, H), jnp.float32) * INIT_STD
        return {'x': x, 'router_w': router_w, 'w1': w1, 'w2': w2}
    _L0_ffn_all = _L0_ffn_setup()
    _L0_ffn_in = {k: v for k, v in _L0_ffn_all.items() if k in ('router_w', 'w1', 'w2')}
    del _L0_ffn_all
    return {'x': x, 'L0_tok_emb_weight': _L0_tok_in['emb_weight'], 'L0_tok_lora_A': _L0_tok_in['lora_A'], 'L0_tok_lora_B': _L0_tok_in['lora_B'], 'L0_attn_Wqkv': _L0_attn_in['Wqkv'], 'L0_attn_bqkv': _L0_attn_in['bqkv'], 'L0_attn_Wout': _L0_attn_in['Wout'], 'L0_attn_bout': _L0_attn_in['bout'], 'L0_attn_Wg': _L0_attn_in['Wg'], 'L0_attn_bg': _L0_attn_in['bg'], 'L0_ffn_router_w': _L0_ffn_in['router_w'], 'L0_ffn_w1': _L0_ffn_in['w1'], 'L0_ffn_w2': _L0_ffn_in['w2']}

def reference(x, L0_tok_emb_weight, L0_tok_lora_A, L0_tok_lora_B, L0_attn_Wqkv, L0_attn_bqkv, L0_attn_Wout, L0_attn_bout, L0_attn_Wg, L0_attn_bg, L0_ffn_router_w, L0_ffn_w1, L0_ffn_w2):
    import jax
    import jax.numpy as jnp

    def _L0_tok_ref(input, emb_weight, lora_A, lora_B):
        import jax, jax.numpy as jnp
        import numpy as np
        VOCAB = 50257
        DIM = 256
        R = 16
        ALPHA = 32
        SCALING = ALPHA / R
        orig_out = jnp.take(emb_weight, input, axis=0)
        a_rows = jnp.take(lora_A, input, axis=1)
        a_rows = jnp.moveaxis(a_rows, 0, -1)
        lora_out = jnp.einsum('bsr,dr->bsd', a_rows, lora_B) * SCALING
        return orig_out + lora_out

    def _L0_attn_ref(hidden_states, Wqkv, bqkv, Wout, bout, Wg, bg):
        import jax, jax.numpy as jnp
        import numpy as np
        B, T, D, H = (1, 1024, 256, 16)
        HD = D // H
        W_LOCAL = 64
        N_GLOBAL = 64
        b, t, d = hidden_states.shape
        scale = 1.0 / jnp.sqrt(jnp.asarray(HD, hidden_states.dtype))
        qkv = hidden_states @ Wqkv + bqkv
        q, k, v = jnp.split(qkv, 3, axis=-1)
        q, k, v = (x.reshape(b, t, H, HD).transpose(0, 2, 1, 3) for x in (q, k, v))
        idx = jnp.arange(t)
        local_mask = jnp.abs(idx[None, :] - idx[:, None]) <= W_LOCAL
        scores = jnp.einsum('bhqd,bhkd->bhqk', q, k) * scale
        scores = jnp.where(local_mask[None, None], scores, -jnp.inf)
        attn_local = jnp.einsum('bhqk,bhkd->bhqd', jax.nn.softmax(scores, axis=-1), v)
        ng = min(N_GLOBAL, t)
        k_g = k[:, :, :ng, :]
        v_g = v[:, :, :ng, :]
        scores_g = jnp.einsum('bhqd,bhgd->bhqg', q, k_g) * scale
        attn_global = jnp.einsum('bhqg,bhgd->bhqd', jax.nn.softmax(scores_g, axis=-1), v_g)
        gate = jax.nn.sigmoid(hidden_states @ Wg + bg).reshape(b, 1, t, 1)
        out = (1.0 - gate) * attn_local + gate * attn_global
        out = out.transpose(0, 2, 1, 3).reshape(b, t, d)
        return out @ Wout + bout

    def _L0_ffn_ref(x, router_w, w1, w2):
        import jax, jax.numpy as jnp
        import numpy as np
        NUM_EXPERTS = 8
        TOP_K = 2
        CAP_RATIO = 1.25
        INIT_STD = 0.02
        B, T, H = x.shape
        E, K = (NUM_EXPERTS, TOP_K)
        xf = x.reshape(-1, H)
        N = xf.shape[0]
        P = N * K
        capacity = int(CAP_RATio * N * K / E) + 1 if False else int(CAP_RATIO * N * K / E) + 1
        logits = xf @ router_w.T
        probs = jax.nn.softmax(logits, axis=-1)
        k_probs, k_idx = jax.lax.top_k(probs, K)
        k_probs = k_probs / jnp.sum(k_probs, axis=-1, keepdims=True)
        flat_e = k_idx.reshape(-1)
        onehot = jax.nn.one_hot(flat_e, E, dtype=jnp.int32)
        rank = jnp.take_along_axis(jnp.cumsum(onehot, axis=0) - 1, flat_e[:, None], axis=1)[:, 0]
        keep = rank < capacity
        slot = jnp.minimum(rank, capacity - 1)
        token_id = jnp.arange(P) // K
        dispatched = jnp.where(keep[:, None], xf[token_id], 0.0)
        buf = jnp.zeros((E, capacity, H), x.dtype).at[flat_e, slot].add(dispatched)
        h = jax.nn.silu(jnp.einsum('ech,ehf->ecf', buf, w1))
        out_buf = jnp.einsum('ecf,efh->ech', h, w2)
        pair_out = out_buf[flat_e, slot] * keep[:, None].astype(x.dtype)
        combined = jnp.sum(pair_out.reshape(N, K, H) * k_probs[..., None], axis=1)
        return combined.reshape(B, T, H) + x
    h = _L0_tok_ref(x, L0_tok_emb_weight, L0_tok_lora_A, L0_tok_lora_B)
    h = h + _L0_attn_ref(_layernorm(h, axis=-1), L0_attn_Wqkv, L0_attn_bqkv, L0_attn_Wout, L0_attn_bout, L0_attn_Wg, L0_attn_bg)
    h = h + _L0_ffn_ref(_layernorm(h, axis=-1), L0_ffn_router_w, L0_ffn_w1, L0_ffn_w2)
    return h

_drawn_inputs = setup_inputs


def setup_inputs(seed=0):
    import zlib

    import numpy as np

    out = dict(_drawn_inputs(seed))
    spreads = {'L0_attn_bqkv': (0.0, 0.1), 'L0_attn_bout': (0.0, 0.1)}
    factors = {'L0_tok_lora_A': 5.461, 'L0_tok_lora_B': 5.391, 'L0_attn_Wqkv': 6.338, 'L0_attn_Wg': 8.0}
    for name, (base, spread) in spreads.items():
        noise = np.random.default_rng([zlib.crc32(name.encode()), seed]).standard_normal(out[name].shape)
        drawn = base * np.exp(spread * noise) if base else spread * noise
        out[name] = jnp.asarray(drawn.astype(out[name].dtype))
    for name, factor in factors.items():
        out[name] = (out[name] * factor).astype(out[name].dtype)
    return out
```

```python
from contextlib import ExitStack

import numpy as np
import concourse.bass as bass
from concourse import mybir

F32 = mybir.dt.float32
F32R = mybir.dt.float32r
BF16 = mybir.dt.bfloat16
I32 = mybir.dt.int32
U32 = mybir.dt.uint32
ALU = mybir.AluOpType
ACT = mybir.ActivationFunctionType
AX = mybir.AxisListType

P = 128
D = 256
KT = D // P
H = 16
HD = D // H
PAIRS = H // 2
DUOS = PAIRS // 2
T = 512
QB = T // P
KB = T // 64
R = 16
E = 8
F = 1024
FT = F // P
EPS = 1e-5
LORA_SCALE = 2.0
SCALE = HD ** -0.5
MASKED = -1e30
VG = 8
M_JOBS = PAIRS * (QB + 1)
E_JOBS = PAIRS * (KB // 2 + 1)


class Link:

    def __init__(self, eng, sem, n, turn):
        self.eng, self.sem, self.n, self.turn, self.k = eng, sem, n, turn, 0

    def __call__(self, ins):
        self.k += 1
        ins.then_inc(self.sem, 1)
        self.eng.wait_ge(self.sem, self.n * self.turn + self.k)

    def end(self):
        assert self.k == self.n, (self.k, self.n)


def build(nc, x, emb, lora_a, lora_b, wqkv, bqkv, wout, bout, wg, bg, rw, w1, w2, y):
    SEQ = x.shape[0]
    N = SEQ * T
    VOCAB = emb.shape[0]
    TOKT = N // P
    CAP = int(1.25 * N * 2 / E) + 1
    HE = -(-CAP // P)
    STRIDE = HE * P
    SLOTS = E * STRIDE
    GT = -(-VOCAB // (VG * P)) * P
    STEPS = GT // P
    GP = PAIRS // 2
    FAR = float(1 << 20)

    lora_rows = nc.dram_tensor("lora_rows", [VG * GT, R], F32, kind="Internal").ap()
    qk_scr = nc.dram_tensor("qk_scr", [2, 2 * D, T], F32, kind="Internal").ap()
    m_scr = nc.dram_tensor("m_scr", [2, 2, H, T], F32, kind="Internal").ap()
    x2_rows = nc.dram_tensor("x2_rows", [N + P, D], F32, kind="Internal").ap()
    table = nc.dram_tensor("slot_table", [SLOTS, 2], I32, kind="Internal").ap()

    outer = ExitStack()
    with outer:
        def sb(ctx, name, shape, dt=F32):
            return ctx.enter_context(nc.sbuf_tensor(name, shape, dt))

        def sem(name):
            return outer.enter_context(nc.semaphore(name))

        psS = outer.enter_context(nc.psum_tensor("psS", [P, 4, 512], F32))
        psO = outer.enter_context(nc.psum_tensor("psO", [P, 2, 512], F32))
        psX = outer.enter_context(nc.psum_tensor("psX", [P, 2, 512], F32))

        ident = sb(outer, "ident", [P, P])
        counts = sb(outer, "counts", [P, E], BF16)
        onesb = sb(outer, "onesb", [P, P], BF16)

        attn_mem = ExitStack()
        outer.enter_context(attn_mem)
        keep = lambda name, shape, dt=F32: sb(attn_mem, name, shape, dt)
        identb = keep("identb", [P, P], BF16)
        upper = keep("upper", [P, P], BF16)
        ids = keep("ids", [P, TOKT], I32)
        mask_q = keep("mask_q", [P, 4, 2, 64], BF16)
        mask_k = keep("mask_k", [P, 2, 2, 64], BF16)
        wqkv_sb = keep("wqkv_sb", [P, KT, 3 * D])
        wout_sb = keep("wout_sb", [P, KT, D])
        wg_sb = keep("wg_sb", [P, KT])
        rw_t = keep("rw_t", [P, KT, E])
        lb_t = keep("lb_t", [R, D])
        wqk = keep("wqk", [P, KT, 4, P])
        bqk = keep("bqk", [P, 4])
        bv = keep("bv", [P, PAIRS, HD])
        bout_b = keep("bout_b", [P, D])
        neg_bg = keep("neg_bg", [P, 1])
        eps_b = keep("eps_b", [P, 1])
        iota8 = keep("iota8", [P, E])
        tokid = keep("tokid", [P, QB])
        zrows = keep("zrows", [4, T])
        Q = keep("Q", [P, PAIRS, T], F32R)
        K = keep("K", [P, PAIRS, KB, 2, 64], F32R)
        KG = keep("KG", [P, PAIRS, 2, 64], F32R)
        V = keep("V", [P, KB, PAIRS, 64])

        with ExitStack() as mem:
            tmp = lambda name, shape, dt=F32: sb(mem, name, shape, dt)
            la_src = tmp("la_src", [P, GT])
            la_dst = tmp("la_dst", [P, VG, STEPS, R])
            ids_rows = tmp("ids_rows", [TOKT, P], I32)
            ids_f = tmp("ids_f", [TOKT, P])
            rw_rows = tmp("rw_rows", [E, D])
            bqk_rows = tmp("bqk_rows", [4, P])
            lb_rows = tmp("lb_rows", [P, KT, R])
            bg_b = tmp("bg_b", [P, 1])
            rowsel = tmp("rowsel", [P, 2, 2])
            tab_i = tmp("tab_i", [P, SLOTS // P], I32)
            tab = tmp("tab", [P, SLOTS // P, 2], I32)
            zpad = tmp("zpad", [P, D])
            weights_in, small_in, lora_in = sem("weights_in"), sem("small_in"), sem("lora_in")
            pool_base, pool_sel = sem("pool_base"), sem("pool_sel")
            dve_base, dve_made = sem("dve_base"), sem("dve_made")
            pe_small, dve_small = sem("pe_small"), sem("dve_small")
            step_ready, step_copied = sem("step_ready"), sem("step_copied")
            scratch_out = sem("scratch_out")
            POOL_SEL = 11
            chunks = [(s, min(4, STEPS - s)) for s in range(0, STEPS, 4)]

            with nc.Block() as block:
                @block.sync
                def _(sp):
                    sp.dma_start(ids_rows[:, :], x.rearrange("s (c p) -> (s c) p", p=P)).then_inc(small_in, 16)
                    sp.dma_start(rw_rows[:, :], rw).then_inc(small_in, 16)
                    sp.dma_start(lb_rows[:, :, :], lora_b.rearrange("(k p) r -> p k r", p=P)).then_inc(small_in, 16)
                    sp.dma_start(bg_b[:, :], bg.rearrange("(a n) -> a n", a=1).to_broadcast([P, 1])).then_inc(small_in, 16)
                    sp.wait_ge(dve_base, 1)
                    for g in range(VG):
                        n = min(GT, VOCAB - g * GT)
                        sp.dma_start(la_src[R * g:R * (g + 1), 0:n], lora_a[:, g * GT:g * GT + n]).then_inc(lora_in, 16)
                    sp.wait_ge(dve_made, 3)
                    sp.dma_start(table.rearrange("(p j) w -> p j w", p=P), tab[:, :, :]).then_inc(scratch_out, 16)
                    sp.dma_start(x2_rows[N:N + P, :], zpad[:, :]).then_inc(scratch_out, 16)
                    sp.dma_start(y[N:N + P, :], zpad[:, :]).then_inc(scratch_out, 16)
                    sp.wait_ge(step_copied, len(chunks))
                    for g in range(VG):
                        sp.dma_start(lora_rows[g * GT:(g + 1) * GT, :].rearrange("(p s) r -> p s r", p=P),
                                     la_dst[:, g, :, :]).then_inc(scratch_out, 16)
                    sp.wait_ge(scratch_out, 16 * (3 + VG))

                @block.scalar
                def _(act):
                    act.dma_start(wqkv_sb[:, :, :], wqkv.rearrange("(k p) n -> p k n", p=P)).then_inc(weights_in, 16)
                    act.dma_start(wout_sb[:, :, :], wout.rearrange("(k p) n -> p k n", p=P)).then_inc(weights_in, 16)
                    act.dma_start(wg_sb[:, :], wg.rearrange("(k p) n -> p (k n)", p=P),
                                  allow_slow_non_contiguous=True).then_inc(weights_in, 16)
                    for s in range(2):
                        for a in range(2):
                            act.dma_start(bqk_rows[2 * s + a:2 * s + a + 1, :].rearrange("o (d h) -> o d h", d=HD),
                                          bqkv[s * D:(s + 1) * D].rearrange("(o h a d) -> a o d h", o=1, a=2, d=HD)[a],
                                          allow_slow_non_contiguous=True).then_inc(weights_in, 16)
                    bvv = bqkv[2 * D:3 * D].rearrange("(o p a d) -> o a p d", o=1, a=2, d=HD)
                    for a in range(2):
                        act.dma_start(bv[64 * a:64 * (a + 1), :, :],
                                      bvv[:, a, :, :].to_broadcast([64, PAIRS, HD])).then_inc(weights_in, 16)
                    act.dma_start(bout_b[:, :],
                                  bout.rearrange("(a n) -> a n", a=1).to_broadcast([P, D])).then_inc(weights_in, 16)
                    act.wait_ge(weights_in, 16 * 10)

                @block.gpsimd
                def _(pool):
                    pool.iota(iota8[:, :], [[1, E]], base=0, channel_multiplier=0,
                              allow_small_or_imprecise_dtypes=True).then_inc(pool_base, 1)
                    pool.wait_ge(pool_base, 1)
                    pool.iota(tokid[:, :], [[P, QB]], base=0, channel_multiplier=1,
                              allow_small_or_imprecise_dtypes=True).then_inc(pool_base, 1)
                    pool.wait_ge(pool_base, 2)
                    pool.iota(tab_i[:, :], [[1, SLOTS // P]], base=0, channel_multiplier=SLOTS // P).then_inc(pool_base, 1)
                    pool.wait_ge(dve_base, 2)
                    made = [0]

                    def select(ap, op, fill, base, pattern, per_row):
                        pool.affine_select(out=ap, in_=ap, compare_op=op, fill=fill, base=base, pattern=pattern,
                                           channel_multiplier=per_row).then_inc(pool_sel, 1)
                        made[0] += 1
                        pool.wait_ge(pool_sel, made[0])

                    for m in (ident, identb):
                        select(m[:, :], ALU.not_equal, 1.0, 0, [[-1, P]], 1)
                    select(upper[:, :], ALU.is_gt, 0.0, 0, [[1, P]], -1)
                    select(mask_q[:, :, :, :], ALU.is_ge, MASKED, 0, [[64, 4], [0, 2], [1, 64]], -1)
                    select(mask_q[:, :, :, :], ALU.is_ge, MASKED, P, [[-64, 4], [0, 2], [-1, 64]], 1)
                    for a in range(2):
                        rows = slice(64 * a, 64 * (a + 1))
                        select(mask_k[rows, :, 0, :], ALU.is_ge, MASKED, 0, [[0, 2], [1, 64]], -1)
                        select(mask_k[rows, :, 1, :], ALU.is_ge, MASKED, 0, [[0, 2], [-1, 64]], 1)
                    for first in (48, 50):
                        select(rowsel[:, :, :], ALU.not_equal, 1.0, -first, [[-1, 2], [-64, 2]], 1)
                    assert made[0] == POOL_SEL

                @block.vector
                def _(dve):
                    dve.memset(la_src[P - 32:P, VOCAB - (VG - 1) * GT:GT], 0.0).then_inc(dve_base, 1)
                    for m in (ident, identb):
                        dve.memset(m[:, :], 0.0)
                    dve.memset(upper[:, :], 1.0)
                    dve.memset(onesb[:, :], 1.0)
                    dve.memset(mask_q[:, :, :, :], 0.0)
                    dve.memset(mask_k[:, :, :, :], 0.0)
                    dve.memset(rowsel[:, :, :], 0.0).then_inc(dve_base, 1)
                    dve.memset(zpad[:, :], 0.0)
                    dve.memset(tab[:, :, :], 0)
                    dve.memset(counts[:, :], 0.0)
                    dve.memset(eps_b[:, :], EPS)
                    dve.memset(zrows[:, :], 0.0)
                    dve.memset(Q[:, :, :].bitcast(F32), 0.0)
                    dve.memset(KG[:, :, :, :].bitcast(F32), 0.0)
                    dve.memset(K[:, :, :, :, :].bitcast(F32), 0.0)
                    dve.memset(V[:, :, :, :], 0.0).then_inc(dve_made, 1)
                    dve.wait_ge(pool_base, 3)
                    dve.tensor_scalar(tab_i[:, :], tab_i[:, :], P - 1, None, ALU.bitwise_and).then_inc(dve_made, 1)
                    dve.wait_ge(dve_made, 2)
                    dve.tensor_scalar(tab[:, :, 0], tab_i[:, :], float(N), None, ALU.add).then_inc(dve_made, 1)
                    dve.memset(V[0:64, :, :, 16:32], 1.0)
                    dve.memset(V[64:P, :, :, 48:64], 1.0)
                    dve.wait_ge(pool_sel, POOL_SEL)
                    for a in range(2):
                        dve.tensor_scalar(K[:, :, :, a, :], K[:, :, :, a, :].bitcast(F32), rowsel[:, 0, a:a + 1], None, ALU.add)
                        dve.tensor_scalar(KG[:, :, a, :], KG[:, :, a, :].bitcast(F32), rowsel[:, 1, a:a + 1], None, ALU.add)
                    dve.wait_ge(weights_in, 16 * 10)
                    for k in range(KT):
                        for s in range(2):
                            dve.tensor_copy(wqk[:, k, 2 * s:2 * s + 2, :].rearrange("p a (d h) -> p a d h", d=HD),
                                            wqkv_sb[:, k, s * D:(s + 1) * D].rearrange("p (h a d) -> p a d h", a=2, d=HD))
                    dve.wait_ge(small_in, 64)
                    dve.tensor_scalar(neg_bg[:, :], bg_b[:, :], -1.0, None, ALU.mult)
                    dve.tensor_copy(ids_f[:, :], ids_rows[:, :]).then_inc(dve_small, 1)
                    dve.wait_ge(pe_small, 1)
                    dve.tensor_copy(ids[:, :], psO[:, 0, 0:TOKT])
                    dve.tensor_copy(rw_t[:, :, :], psO[:, 0, 256:256 + KT * E].rearrange("p (k e) -> p k e", k=KT))
                    dve.tensor_copy(lb_t[:, :], psO[0:R, 1, 0:D])
                    dve.tensor_copy(bqk[:, :], psO[:, 0, 300:304])
                    for c, (s, n) in enumerate(chunks):
                        dve.wait_ge(step_ready, c + 1)
                        dve.tensor_copy(la_dst[:, :, s:s + n, :],
                                        psX[:, c % 2, 0:n * P].rearrange("p (s g r) -> p g s r", s=n, g=VG)).then_inc(step_copied, 1)

                @block.tensor
                def _(pe):
                    pe.wait_ge(pool_sel, 1)
                    pe.wait_ge(small_in, 64)
                    pe.wait_ge(dve_small, 1)
                    pe.transpose(psO[:, 0, 0:TOKT], ids_f[:, :], ident[0:TOKT, 0:TOKT])
                    for k in range(KT):
                        pe.transpose(psO[:, 0, 256 + k * E:256 + (k + 1) * E], rw_rows[:, k * P:(k + 1) * P], ident[0:E, 0:E])
                    for k in range(KT):
                        pe.transpose(psO[0:R, 1, k * P:(k + 1) * P], lb_rows[:, k, :], ident[:, :])
                    pe.wait_ge(weights_in, 16 * 10)
                    pe.transpose(psO[:, 0, 300:304], bqk_rows[:, :], ident[0:4, 0:4]).then_inc(pe_small, 1)
                    pe.wait_ge(lora_in, 16 * VG)
                    for c, (s, n) in enumerate(chunks):
                        if c >= 2:
                            pe.wait_ge(step_copied, c - 1)
                        for j in range(n):
                            last = pe.transpose(psX[:, c % 2, j * P:(j + 1) * P],
                                                la_src[:, s + j:s + j + (P - 1) * STEPS + 1:STEPS], ident[:, :])
                        last.then_inc(step_ready, 1)

        with ExitStack() as mem:
            tmp = lambda name, shape, dt=F32: sb(mem, name, shape, dt)
            id_cur = tmp("id_cur", [P, QB], I32)
            emb_t = tmp("emb_t", [P, QB, D])
            la = tmp("la", [P, QB, R])
            la_t = tmp("la_t", [R, T])
            h = tmp("h", [P, QB, D])
            hb = tmp("hb", [P, QB, D])
            stats1 = tmp("stats1", [P, QB, 6])
            mv1 = tmp("mv1", [P, QB, 2])
            std1 = tmp("std1", [P, QB])
            rstd1 = tmp("rstd1", [P, QB])
            xn = tmp("xn", [P, QB, D])
            xn_t = tmp("xn_t", [P, KT, T])
            egate = tmp("egate", [P, QB])
            egate1 = tmp("egate1", [P, QB])
            gate_new = tmp("gate_new", [P, QB])
            gates = tmp("gates", [P, 2, QB])
            qk_hi = tmp("qk_hi", [P, 4, T], F32R)
            qk_lo = tmp("qk_lo", [P, 4, T], F32R)
            negm = tmp("negm", [P, QB, 2, H])
            m_hi = tmp("m_hi", [2 * H, T], F32R)
            m_lo = tmp("m_lo", [2 * H, T], F32R)
            pl = tmp("pl", [P, 4, KB // 2, 384])
            pg = tmp("pg", [P, 4, T])
            o_t = tmp("o_t", [P, 2, DUOS, T])
            rsum = tmp("rsum", [P, 2, H])
            coef = tmp("coef", [P, 2, H])
            mix = tmp("mix", [P, 2, H, HD])
            attn = tmp("attn", [P, QB, D])
            attn_t = tmp("attn_t", [P, KT, T])
            h1 = tmp("h1", [P, QB, D])
            stats2 = tmp("stats2", [P, QB, 6])
            mv2 = tmp("mv2", [P, QB, 2])
            std2 = tmp("std2", [P, QB])
            rstd2 = tmp("rstd2", [P, QB])
            x2 = tmp("x2", [P, QB, D])
            x2_t = tmp("x2_t", [P, KT, T])
            logit = tmp("logit", [P, QB, E])
            top = tmp("top", [P, QB, 8])
            top_i = tmp("top_i", [P, QB, 8], U32)
            top_f = tmp("top_f", [P, QB, 2])
            gap = tmp("gap", [P, QB])
            egap = tmp("egap", [P, QB])
            egap1 = tmp("egap1", [P, QB])
            prob = tmp("prob", [P, QB, 2])
            onehot = tmp("onehot", [P, QB, 2, E])
            chosen = tmp("chosen", [P, QB, E], BF16)
            before = tmp("before", [P, QB + 1, E], BF16)
            ahead = tmp("ahead", [P, QB, E])
            picked = tmp("picked", [P, QB, 2, E])
            rank = tmp("rank", [P, QB, 2])
            over = tmp("over", [P, QB, 2])
            slot = tmp("slot", [P, QB, 2])
            slot_i = tmp("slot_i", [P, QB, 2], I32)
            entry = tmp("entry", [P, QB, 2, 2], I32)

            id_ready, rows_in = sem("id_ready"), sem("rows_in")
            la_t_ready, la_t_done, lora_ready = sem("la_t_ready"), sem("la_t_done"), sem("lora_ready")
            h_done, mv1_done, std1_done, xn_done = sem("h_done"), sem("mv1_done"), sem("std1_done"), sem("xn_done")
            xn_t_ready, xn_t_done = sem("xn_t_ready"), sem("xn_t_done")
            qk_ready, qk_hi_done, qk_lo_done = sem("qk_ready"), sem("qk_hi_done"), sem("qk_lo_done")
            gate_ready, egate_done = sem("gate_ready"), sem("egate_done")
            v_ready, v_done = sem("v_ready"), sem("v_done")
            qk_out = sem("qk_out")
            half_in = [sem("half0_in"), sem("half1_in")]
            s_ready, max_done = sem("s_ready"), sem("max_done")
            m_t_ready, m_hi_done, m_lo_done = sem("m_t_ready"), sem("m_hi_done"), sem("m_lo_done")
            m_out, m_in = sem("m_out"), sem("m_in")
            st_ready, exp_done = sem("st_ready"), sem("exp_done")
            ol_ready, og_ready, ol_done, og_done = sem("ol_ready"), sem("og_ready"), sem("ol_done"), sem("og_done")
            o_ready, o_read, attn_done = sem("o_ready"), sem("o_read"), sem("attn_done")
            attn_t_ready, attn_t_done = sem("attn_t_ready"), sem("attn_t_done")
            wout_ready, h1_done = sem("wout_ready"), sem("h1_done")
            mv2_done, std2_done, x2_done = sem("mv2_done"), sem("std2_done"), sem("x2_done")
            x2_t_ready, x2_t_done = sem("x2_t_ready"), sem("x2_t_done")
            logit_ready, logit_done, gap_done, egap_done = sem("logit_ready"), sem("logit_done"), sem("gap_done"), sem("egap_done")
            chosen_done, ahead_ready, ahead_done, entry_done = sem("chosen_done"), sem("ahead_ready"), sem("ahead_done"), sem("entry_done")
            res_done, y_out, x2_out, entry_out = sem("res_done"), sem("y_out"), sem("x2_out"), sem("entry_out")
            k_ln1, k_ln2, k_top, k_rank, k_mix, k_hb = (sem("k_ln1"), sem("k_ln2"), sem("k_top"), sem("k_rank"),
                                                        sem("k_mix"), sem("k_hb"))
            HALF_DMAS = 20 * 16
            carry = {"sp": sem("sp_carry"), "pool": sem("pool_carry"), "dve": sem("dve_carry")}

            def turns(eng, turn):
                turn(-1, False, False, True)
                turn(0, False, True, True)
                turn(1, True, True, True)
                with eng.Fori(2, SEQ - 1) as i:
                    turn(i, True, True, True)
                turn(SEQ - 1, True, True, False)
                turn(SEQ, True, False, False)

            def keys_of(qb):
                lo, hi = max(0, 2 * qb - 1), min(KB, 2 * qb + 3)
                return lo, hi, lo - (2 * qb - 1)

            class Bank:
                def __init__(self):
                    self.last = [None, None]

                def take(self, pe, b, i, signal, per, k, rel):
                    if self.last[b] is not None:
                        s, p_, k_, r_ = self.last[b]
                        pe.wait_ge(s, p_ * (i + r_) + k_)
                    self.last[b] = (signal, per, k, rel)

                def next_turn(self):
                    self.last = [x and (*x[:3], x[3] - 1) for x in self.last]

            with nc.Block() as block:
                @block.gpsimd
                def _(pool):
                    def turn(i, prev, cur, nxt):
                        if nxt:
                            if cur:
                                pool.wait_ge(rows_in, 2 * QB * 16 * (i + 1))
                                pool.wait_ge(h_done, 2 * (i + 1))
                            pool.tensor_copy(id_cur[:, :], ids[:, bass.ts(i + 1, QB)]).then_inc(id_ready, 1)
                            pool.wait_ge(id_ready, i + 2)
                            pool.sem_inc(carry["pool"], 1)
                            for q in range(QB):
                                at = bass.IndirectOffsetOnAxis(ap=id_cur[:, q:q + 1], axis=0)
                                pool.indirect_dma_start(out=la[:, q, :], out_offset=None, in_=lora_rows[:, :],
                                                        in_offset=at).then_inc(rows_in, 16)
                                pool.indirect_dma_start(out=emb_t[:, q, :], out_offset=None, in_=emb[:, :],
                                                        in_offset=at).then_inc(rows_in, 16)
                        if prev:
                            pool.wait_ge(x2_done, QB * i)
                            pool.tensor_tensor(h1[:, :, :], h1[:, :, :], x2[:, :, :], ALU.add).then_inc(res_done, 1)
                            pool.wait_ge(entry_done, i)
                            pool.sem_inc(carry["pool"], 1)
                            for q in range(QB):
                                for k in range(2):
                                    pool.indirect_dma_start(
                                        out=table[:, :], in_=entry[:, q, k, :], in_offset=None,
                                        out_offset=bass.IndirectOffsetOnAxis(ap=slot_i[:, q, k:k + 1], axis=0),
                                        bounds_check=SLOTS - 1, oob_is_err=False).then_inc(entry_out, 16)
                    turns(pool, turn)
                    pool.wait_ge(entry_out, 2 * QB * 16 * SEQ)

                @block.sync
                def _(sp):
                    y_seq = y[0:N, :].rearrange("(s q p) d -> s p q d", q=QB, p=P)
                    x2_seq = x2_rows[0:N, :].rearrange("(s q p) d -> s p q d", q=QB, p=P)

                    def turn(i, prev, cur, nxt):
                        if cur:
                            sp.wait_ge(m_hi_done, i + 1)
                            sp.sem_inc(carry["sp"], 1)
                            sp.wait_ge(m_lo_done, i + 1)
                            sp.sem_inc(carry["sp"], 1)
                            if prev:
                                sp.wait_ge(m_in, 32 * i)
                            sp.dma_start(m_scr[0].rearrange("k h t -> (k h) t"), m_hi[:, :].bitcast(F32)).then_inc(m_out, 16)
                            sp.dma_start(m_scr[1].rearrange("k h t -> (k h) t"), m_lo[:, :].bitcast(F32)).then_inc(m_out, 16)
                            sp.wait_ge(m_out, 32 * (i + 1))
                            for a in range(2):
                                sp.dma_start(Q[64 * a + 48:64 * a + 52, :, :].bitcast(F32),
                                             m_scr.rearrange("l k (p a) t -> a (l k) p t", a=2)[a]).then_inc(m_in, 16)
                        if prev:
                            sp.wait_ge(x2_done, QB * i)
                            sp.dma_start(x2_seq[i - 1], x2[:, :, :]).then_inc(x2_out, 16)
                            sp.wait_ge(res_done, i)
                            sp.dma_start(y_seq[i - 1], h1[:, :, :]).then_inc(y_out, 16)
                        if nxt:
                            sp.wait_ge(qk_hi_done, 4 * (i + 2))
                            sp.sem_inc(carry["sp"], 1)
                            sp.wait_ge(qk_lo_done, 4 * (i + 2))
                            sp.sem_inc(carry["sp"], 1)
                            if cur:
                                for g in range(2):
                                    sp.wait_ge(half_in[g], HALF_DMAS * (i + 1))
                            for l, rows in enumerate((qk_hi, qk_lo)):
                                sp.dma_start(qk_scr[l].rearrange("(g p) t -> p g t", p=P),
                                             rows[:, :, :].bitcast(F32)).then_inc(qk_out, 16)
                            sp.wait_ge(qk_out, 32 * (i + 2))
                            for g in range(2):
                                if cur:
                                    sp.wait_ge(st_ready, E_JOBS * i + E_JOBS // 2 * (g + 1))
                                half = slice(GP * g, GP * (g + 1))
                                src = qk_scr.rearrange("l (s a d p) t -> s l a d p t", s=2, a=2, d=HD)
                                for a in range(2):
                                    for j, (lq, lk) in enumerate(((0, 0), (1, 0), (0, 1))):
                                        rows = slice(64 * a + HD * j, 64 * a + HD * (j + 1))
                                        sp.dma_start(Q[rows, half, :].bitcast(F32), src[0, lq, a][:, half]).then_inc(half_in[g], 16)
                                        keys = src[1, lk, a][:, half]
                                        sp.dma_start(K[rows, half, :, a, :].rearrange("d p k c -> d (p k) c").bitcast(F32),
                                                     keys.rearrange("d p (k c) -> d (p k) c", c=64)).then_inc(half_in[g], 16)
                                        sp.dma_start(KG[rows, half, a, :].bitcast(F32), keys[:, :, 0:64]).then_inc(half_in[g], 16)
                                    sp.dma_start(Q[64 * a + 48:64 * a + 52, half, :].bitcast(F32), zrows[:, :].unsqueeze(1).to_broadcast([4, GP, T])).then_inc(half_in[g], 16)
                    turns(sp, turn)
                    sp.wait_ge(x2_out, 16 * SEQ)
                    sp.wait_ge(y_out, 16 * SEQ)

                @block.tensor
                def _(pe):
                    bank = Bank()

                    def max_pass(i, half):
                        pe.wait_ge(half_in[half], HALF_DMAS * (i + 1))
                        for pr in range(GP * half, GP * (half + 1)):
                            for q in range(QB + 1):
                                n = pr * (QB + 1) + q
                                if n >= 4:
                                    pe.wait_ge(max_done, M_JOBS * i + n - 3)
                                elif not (isinstance(i, int) and i == 0):
                                    pe.wait_ge(exp_done, E_JOBS * (i - 1) + E_JOBS - 3 + n)
                                out = psS[:, n % 4, :]
                                if q < QB:
                                    lo, hi, w = keys_of(q)
                                    cols = (hi - lo) * P
                                    pe.matmul(out[:, 0:cols], identb[:, :], mask_q[:, w:w + hi - lo, :, :],
                                              start=True, stop=False)
                                    last = pe.matmul(out[:, 0:cols], Q[:, pr, q * P:(q + 1) * P], K[:, pr, lo:hi, :, :],
                                                     start=False, stop=True)
                                else:
                                    for b in range(QB):
                                        last = pe.matmul(out[:, b * P:(b + 1) * P], Q[:, pr, b * P:(b + 1) * P],
                                                         KG[:, pr, :, :], start=True, stop=True)
                                last.then_inc(s_ready, 1)

                    def out_chunk(i, duo, c):
                        if c == 0:
                            pe.wait_ge(exp_done, E_JOBS * i + 10 * (duo + 1))
                            if not (isinstance(i, int) and i == 0 and duo == 0):
                                pe.wait_ge(ol_done, DUOS * i + duo)
                        if c == KB and not (isinstance(i, int) and i == 0 and duo == 0):
                            pe.wait_ge(og_done, DUOS * i + duo)
                        for s in range(2):
                            pr = 2 * duo + s
                            rows = slice(64 * s, 64 * (s + 1))
                            if c < KB:
                                lo, hi = max(0, 64 * c - 64), min(T, 64 * c + P)
                                at = (c % 2) * 192 + (64 if c == 0 else 0)
                                last = pe.matmul(psO[rows, 0, lo:hi], V[:, c, pr, :], pl[:, pr % 4, c // 2, at:at + hi - lo],
                                                 start=(c == 0), stop=(c == KB - 1), skip_group_check=True)
                            else:
                                last = pe.matmul(psO[rows, 1, :], V[:, 0, pr, :], pg[:, pr % 4, :], start=True, stop=True)
                        if c == KB - 1:
                            last.then_inc(ol_ready, 1)
                        if c == KB:
                            last.then_inc(og_ready, 1)

                    def score_tile(i, n):
                        pr, j = divmod(n, KB // 2 + 1)
                        if n >= 4:
                            pe.wait_ge(exp_done, E_JOBS * i + n - 3)
                        else:
                            pe.wait_ge(max_done, M_JOBS * i + M_JOBS - 3 + n)
                        out = psS[:, n % 4, :]
                        if j < KB // 2:
                            for s in range(2):
                                kb = 2 * j + s
                                lo, hi = max(0, 64 * kb - 64), min(T, 64 * kb + P)
                                at = s * 192 + (64 if kb == 0 else 0)
                                pe.matmul(out[:, at:at + hi - lo], K[:, pr, kb, :, :], Q[:, pr, lo:hi],
                                          start=(s == 0), stop=False, skip_group_check=True)
                            parts = out[:, 0:384].rearrange("p (s l c) -> p s l c", s=2, c=64)[:, :, 0:3:2, :]
                            if j == 0:
                                pe.matmul(parts[:, 0, 1, :], identb[:, :], mask_k[:, 0, 1, :], start=False, stop=False,
                                          skip_group_check=True)
                                last = pe.matmul(parts[:, 1, :, :], identb[:, :], mask_k[:, 1, :, :], start=False, stop=True,
                                                 skip_group_check=True)
                            elif j == KB // 2 - 1:
                                pe.matmul(parts[:, 0, :, :], identb[:, :], mask_k[:, 0, :, :], start=False, stop=False,
                                          skip_group_check=True)
                                last = pe.matmul(parts[:, 1, 0, :], identb[:, :], mask_k[:, 1, 0, :], start=False, stop=True,
                                                 skip_group_check=True)
                            else:
                                last = pe.matmul(parts, identb[:, :], mask_k[:, :, :, :], start=False, stop=True,
                                                 skip_group_check=True)
                        else:
                            last = pe.matmul(out, KG[:, pr, :, :], Q[:, pr, :], start=True, stop=True)
                        last.then_inc(st_ready, 1)

                    def turn(i, prev, cur, nxt):
                        def take(b, signal, per, k, rel):
                            bank.take(pe, b, i, signal, per, k, rel)

                        if cur:
                            max_pass(i, 0)
                        if prev:
                            pe.wait_ge(attn_done, QB * i)
                            for k in range(KT):
                                take(k, attn_t_done, KT, k + 1, -1)
                                for q in range(QB):
                                    last = pe.transpose(psX[:, k, q * P:(q + 1) * P], attn[:, q, k * P:(k + 1) * P], ident[:, :])
                                last.then_inc(attn_t_ready, 1)
                        if cur:
                            max_pass(i, 1)
                        if prev:
                            pe.wait_ge(attn_t_done, KT * i)
                            for j in range(2):
                                take(j, h1_done, 2, j + 1, -1)
                                for q in (2 * j, 2 * j + 1):
                                    for k in range(KT):
                                        last = pe.matmul(psX[:, j, (q % 2) * D:(q % 2 + 1) * D], attn_t[:, k, q * P:(q + 1) * P],
                                                         wout_sb[:, k, :], start=(k == 0), stop=(k == KT - 1))
                                last.then_inc(wout_ready, 1)
                        if nxt:
                            pe.wait_ge(rows_in, 2 * QB * 16 * (i + 2))
                            take(0, la_t_done, 1, 1, 1)
                            for q in range(QB):
                                last = pe.transpose(psX[0:R, 0, q * P:(q + 1) * P], la[:, q, :], ident[:, :])
                            last.then_inc(la_t_ready, 1)
                            pe.wait_ge(la_t_done, i + 2)
                            for j in range(2):
                                take(1 - j, h_done, 2, j + 1, 1)
                                for q in (2 * j, 2 * j + 1):
                                    last = pe.matmul(psX[:, 1 - j, (q % 2) * D:(q % 2 + 1) * D], la_t[:, q * P:(q + 1) * P],
                                                     lb_t[:, :], start=True, stop=True)
                                last.then_inc(lora_ready, 1)
                        if cur:
                            pe.wait_ge(max_done, M_JOBS * (i + 1))
                            take(1, m_lo_done, 1, 1, 0)
                            for q in range(QB):
                                last = pe.transpose(psX[0:2 * H, 1, q * P:(q + 1) * P],
                                                    negm[:, q, :, :].rearrange("p k h -> p (k h)"), ident[:, :])
                            last.then_inc(m_t_ready, 1)
                        if nxt:
                            pe.wait_ge(xn_done, QB * (i + 2))
                            for k in range(KT):
                                take(k, xn_t_done, KT, k + 1, 1)
                                for q in range(QB):
                                    last = pe.transpose(psX[:, k, q * P:(q + 1) * P], xn[:, q, k * P:(k + 1) * P], ident[:, :])
                                last.then_inc(xn_t_ready, 1)
                        if prev:
                            pe.wait_ge(x2_done, QB * i)
                            for k in range(KT):
                                take(k, x2_t_done, KT, k + 1, -1)
                                for q in range(QB):
                                    last = pe.transpose(psX[:, k, q * P:(q + 1) * P], x2[:, q, k * P:(k + 1) * P], ident[:, :])
                                last.then_inc(x2_t_ready, 1)
                        if nxt:
                            pe.wait_ge(xn_t_done, KT * (i + 2))
                            for t in range(4):
                                take(t % 2, qk_lo_done, 4, t + 1, 1)
                                for k in range(KT):
                                    last = pe.matmul(psX[:, t % 2, :], wqk[:, k, t, :], xn_t[:, k, :],
                                                     start=(k == 0), stop=(k == KT - 1))
                                last.then_inc(qk_ready, 1)
                            take(0, egate_done, 1, 1, 1)
                            for q in range(QB):
                                for k in range(KT):
                                    last = pe.matmul(psX[:, 0, q:q + 1], xn_t[:, k, q * P:(q + 1) * P], wg_sb[:, k:k + 1],
                                                     start=(k == 0), stop=(k == KT - 1))
                            last.then_inc(gate_ready, 1)
                        if prev:
                            pe.wait_ge(x2_t_done, KT * i)
                            take(1, logit_done, 1, 1, -1)
                            for q in range(QB):
                                for k in range(KT):
                                    last = pe.matmul(psX[:, 1, q * E:(q + 1) * E], x2_t[:, k, q * P:(q + 1) * P], rw_t[:, k, :],
                                                     start=(k == 0), stop=(k == KT - 1))
                            last.then_inc(logit_ready, 1)
                        if cur:
                            pe.wait_ge(m_in, 32 * (i + 1))
                            pe.wait_ge(v_done, 4 * (i + 1))
                            for n in range(E_JOBS // 2):
                                score_tile(i, n)
                                if n >= 10 and n % 10 <= KB:
                                    out_chunk(i, n // 10 - 1, n % 10)
                        if prev:
                            pe.wait_ge(chosen_done, i)
                            take(0, ahead_done, 1, 1, -1)
                            for q in range(QB):
                                pe.matmul(psX[:, 0, q * E:(q + 1) * E], upper[:, :], chosen[:, q, :], start=True, stop=False)
                                last = pe.matmul(psX[:, 0, q * E:(q + 1) * E], onesb[:, :], before[:, q, :], start=False, stop=True)
                            last.then_inc(ahead_ready, 1)
                        if cur:
                            for n in range(E_JOBS // 2, E_JOBS):
                                score_tile(i, n)
                                if n % 10 <= KB:
                                    out_chunk(i, n // 10 - 1, n % 10)
                            for c in range(KB + 1):
                                out_chunk(i, DUOS - 1, c)
                        if nxt:
                            wv = wqkv_sb[:, :, 2 * D:3 * D].rearrange("p k (h a d) -> p k a h d", a=2, d=HD)
                            for j in range(2):
                                take(1 - j, v_done, 4, 2 * (j + 1), 1)
                                for kb in range(4 * j, 4 * j + 4):
                                    for k in range(KT):
                                        for a in range(2):
                                            last = pe.matmul(psX[64 * a:64 * (a + 1), 1 - j, (kb % 4) * P:(kb % 4 + 1) * P],
                                                             xn_t[:, k, kb * 64:(kb + 1) * 64], wv[:, k, a, :, :],
                                                             start=(k == 0), stop=(k == KT - 1))
                                last.then_inc(v_ready, 1)
                        if cur:
                            pe.wait_ge(ol_done, DUOS * (i + 1))
                            pe.wait_ge(og_done, DUOS * (i + 1))
                            for q in range(QB):
                                for kind in range(2):
                                    take(kind, o_read, QB, q + 1, 0)
                                    for duo in range(DUOS):
                                        last = pe.transpose(psX[:, kind, duo * P:(duo + 1) * P],
                                                            o_t[:, kind, duo, q * P:(q + 1) * P], ident[:, :])
                                last.then_inc(o_ready, 1)
                        bank.next_turn()
                    turns(pe, turn)

                @block.scalar
                def _(act):
                    def turn(i, prev, cur, nxt):
                        if prev:
                            for k in range(KT):
                                act.wait_ge(attn_t_ready, KT * (i - 1) + k + 1)
                                if k == 0:
                                    act.wait_ge(wout_ready, 2 * (i - 1))
                                act.activation(attn_t[:, k, :], psX[:, k, :], ACT.Copy).then_inc(attn_t_done, 1)
                        if nxt:
                            act.wait_ge(la_t_ready, i + 2)
                            if cur:
                                act.wait_ge(lora_ready, 2 * (i + 1))
                            act.activation(la_t[:, :], psX[0:R, 0, :], ACT.Copy).then_inc(la_t_done, 1)
                        if cur:
                            act.wait_ge(m_t_ready, i + 1)
                            if prev:
                                act.wait_ge(m_out, 32 * i)
                                act.wait_ge(m_lo_done, i)
                            act.activation(m_hi[:, :], psX[0:2 * H, 1, :], ACT.Copy).then_inc(m_hi_done, 1)
                        if prev:
                            act.wait_ge(mv2_done, i)
                            act.activation(std2[:, :], mv2[:, :, 1], ACT.Sqrt, bias=eps_b[:, :]).then_inc(std2_done, 1)
                        if nxt:
                            act.wait_ge(mv1_done, i + 2)
                            act.activation(std1[:, :], mv1[:, :, 1], ACT.Sqrt, bias=eps_b[:, :]).then_inc(std1_done, 1)
                            for k in range(KT):
                                act.wait_ge(xn_t_ready, KT * (i + 1) + k + 1)
                                if k == 0 and cur:
                                    act.wait_ge(v_ready, 2 * (i + 1))
                                act.activation(xn_t[:, k, :], psX[:, k, :], ACT.Copy).then_inc(xn_t_done, 1)
                        if prev:
                            for k in range(KT):
                                act.wait_ge(x2_t_ready, KT * (i - 1) + k + 1)
                                if k == 0:
                                    act.wait_ge(logit_ready, i - 1)
                                act.activation(x2_t[:, k, :], psX[:, k, :], ACT.Copy).then_inc(x2_t_done, 1)
                        if nxt:
                            for t in range(4):
                                act.wait_ge(qk_ready, 4 * (i + 1) + t + 1)
                                if t == 0 and cur:
                                    act.wait_ge(qk_out, 32 * (i + 1))
                                    act.wait_ge(qk_lo_done, 4 * (i + 1))
                                act.activation(qk_hi[:, t, :], psX[:, t % 2, :], ACT.Identity,
                                               bias=bqk[:, t:t + 1]).then_inc(qk_hi_done, 1)
                            act.wait_ge(gate_ready, i + 2)
                            act.activation(egate[:, :], psX[:, 0, 0:QB], ACT.Exp, bias=neg_bg[:, :],
                                           scale=-1.0).then_inc(egate_done, 1)
                        if prev:
                            act.wait_ge(gap_done, i)
                            act.activation(egap[:, :], gap[:, :], ACT.Exp).then_inc(egap_done, 1)
                        if cur:
                            def outputs(duo):
                                for kind, ready, done in ((0, ol_ready, ol_done), (1, og_ready, og_done)):
                                    act.wait_ge(ready, DUOS * i + duo + 1)
                                    if prev and duo == 0 and kind == 0:
                                        act.wait_ge(o_ready, QB * i)
                                    act.activation(o_t[:, kind, duo, :], psO[:, kind, :], ACT.Copy).then_inc(done, 1)

                            for n in range(E_JOBS):
                                pr, j = divmod(n, KB // 2 + 1)
                                act.wait_ge(st_ready, E_JOBS * i + n + 1)
                                if pr % 2 == 0 and j == 0 and (prev or pr >= 4):
                                    act.wait_ge(og_ready, DUOS * i + pr // 2 - 1)
                                if j == KB // 2:
                                    act.activation(pg[:, pr % 4, :], psS[:, n % 4, :], ACT.Exp, scale=SCALE).then_inc(exp_done, 1)
                                else:
                                    lo, hi = (64 if j == 0 else 0), (320 if j == KB // 2 - 1 else 384)
                                    act.activation(pl[:, pr % 4, j, lo:hi], psS[:, n % 4, lo:hi], ACT.Exp,
                                                   scale=SCALE).then_inc(exp_done, 1)
                                if n % 10 == 9 and n >= 10:
                                    outputs(n // 10 - 1)
                            outputs(DUOS - 1)
                    turns(act, turn)

                @block.vector
                def _(dve):
                    def route_top(i):
                        link = Link(dve, k_top, 10, i - 1)
                        dve.wait_ge(logit_ready, i)
                        dve.tensor_copy(logit[:, :, :], psX[:, 1, 0:QB * E].rearrange("p (q e) -> p q e", e=E)).then_inc(logit_done, 1)
                        dve.wait_ge(logit_done, i)
                        dve.sem_inc(carry["dve"], 1)
                        for q in range(QB):
                            ins = dve.max(top[:, q, :], logit[:, q, :])
                        link(ins)
                        dve.tensor_tensor(gap[:, :], top[:, :, 1], top[:, :, 0], ALU.subtract).then_inc(gap_done, 1)
                        for q in range(QB):
                            ins = dve.max_index(top_i[:, q, :], top[:, q, :], logit[:, q, :])
                        link(ins)
                        link(dve.tensor_copy(top_f[:, :, :], top_i[:, :, 0:2]))
                        hot = onehot[:, :, :, :].rearrange("p q k e -> p (q k) e")
                        link(dve.tensor_tensor(hot, iota8[:, :].unsqueeze(1).to_broadcast([P, 2 * QB, E]),
                                               top_f[:, :, :].rearrange("p q k -> p (q k)").unsqueeze(2).to_broadcast([P, 2 * QB, E]),
                                               ALU.is_equal))
                        dve.wait_ge(ahead_ready, i - 1)
                        dve.tensor_tensor(chosen[:, :, :], onehot[:, :, 0, :], onehot[:, :, 1, :], ALU.add)
                        link(dve.tensor_copy(before[:, 0, :], counts[:, :]))
                        for q in range(QB):
                            link(dve.tensor_tensor(before[:, q + 1, :], before[:, q, :], chosen[:, q, :], ALU.add))
                        dve.tensor_copy(counts[:, :], before[:, QB, :]).then_inc(chosen_done, 1)
                        dve.wait_ge(egap_done, i)
                        link(dve.tensor_scalar(egap1[:, :], egap[:, :], 1.0, None, ALU.add))
                        link.end()

                    def route_rank(i):
                        link = Link(dve, k_rank, 5, i - 1)
                        link(dve.reciprocal(prob[:, :, 0], egap1[:, :]))
                        dve.tensor_tensor(prob[:, :, 1], egap[:, :], prob[:, :, 0], ALU.mult)
                        dve.wait_ge(ahead_ready, i)
                        dve.tensor_copy(ahead[:, :, :], psX[:, 0, 0:QB * E].rearrange("p (q e) -> p q e", e=E)).then_inc(ahead_done, 1)
                        dve.wait_ge(ahead_done, i)
                        link(dve.tensor_tensor(picked[:, :, :, :], onehot[:, :, :, :],
                                               ahead[:, :, :].unsqueeze(2).to_broadcast([P, QB, 2, E]), ALU.mult))
                        link(dve.tensor_reduce(rank[:, :, :], picked[:, :, :, :], AX.X, ALU.add))
                        dve.tensor_scalar(over[:, :, :], rank[:, :, :], float(CAP), FAR, ALU.is_ge, ALU.mult)
                        link(dve.scalar_tensor_tensor(slot[:, :, :], top_f[:, :, :], float(STRIDE), rank[:, :, :],
                                                      ALU.mult, ALU.add))
                        dve.wait_ge(entry_out, 2 * QB * 16 * (i - 1))
                        dve.tensor_tensor(slot_i[:, :, :], slot[:, :, :], over[:, :, :], ALU.add)
                        dve.tensor_copy(entry[:, :, :, 0], tokid[:, :].unsqueeze(2).to_broadcast([P, QB, 2]))
                        dve.tensor_copy(entry[:, :, :, 1].bitcast(F32), prob[:, :, :]).then_inc(entry_done, 1)
                        dve.wait_ge(entry_done, i)
                        link(dve.tensor_scalar(tokid[:, :], tokid[:, :], float(T), None, ALU.add))
                        link.end()

                    def mixed(i, prev):
                        link = Link(dve, k_mix, 3 * QB, i)
                        outs = psX[:, :, :].rearrange("p k (h w) -> p k h w", w=2 * HD)
                        for q in range(QB):
                            dve.wait_ge(o_ready, QB * i + q + 1)
                            link(dve.reciprocal(rsum[:, :, :], outs[:, :, :, HD]))
                            for kind in range(2):
                                ins = dve.tensor_scalar(coef[:, kind, :], rsum[:, kind, :], gates[:, kind, q:q + 1], None, ALU.mult)
                            link(ins)
                            link(dve.tensor_tensor(mix[:, :, :, :], outs[:, :, :, 0:HD],
                                                   coef[:, :, :].unsqueeze(3).to_broadcast([P, 2, H, HD]), ALU.mult))
                            dve.sem_inc(o_read, 1)
                            if q == 0 and prev:
                                dve.wait_ge(attn_t_ready, KT * i)
                            dve.tensor_tensor(attn[:, q, :].rearrange("p (h d) -> p h d", h=H), mix[:, 0, :, :], mix[:, 1, :, :],
                                              ALU.add).then_inc(attn_done, 1)
                        link.end()

                    def turn(i, prev, cur, nxt):
                        if cur:
                            dve.tensor_scalar(gates[:, 0, :], gate_new[:, :], -1.0, 1.0, ALU.mult, ALU.add)
                            dve.tensor_copy(gates[:, 1, :], gate_new[:, :])
                            for n in range(M_JOBS):
                                pr, q = divmod(n, QB + 1)
                                dve.wait_ge(s_ready, M_JOBS * i + n + 1)
                                if n == 0 and prev:
                                    dve.wait_ge(m_t_ready, i)
                                if q < QB:
                                    lo, hi, _ = keys_of(q)
                                    dve.tensor_reduce(negm[:, q, 0, 2 * pr:2 * pr + 2],
                                                      psS[:, n % 4, 0:(hi - lo) * P].rearrange("p (k a c) -> p a k c", a=2, c=64),
                                                      AX.XY, ALU.max, negate=True).then_inc(max_done, 1)
                                else:
                                    dve.tensor_reduce(negm[:, :, 1, 2 * pr:2 * pr + 2],
                                                      psS[:, n % 4, :].rearrange("p (q a c) -> p q a c", a=2, c=64),
                                                      AX.X, ALU.max, negate=True).then_inc(max_done, 1)
                        if prev:
                            link = Link(dve, k_ln2, 2, i - 1)
                            for j in range(2):
                                dve.wait_ge(wout_ready, 2 * (i - 1) + j + 1)
                                if j == 0:
                                    dve.wait_ge(y_out, 16 * (i - 1))
                                ins = dve.tensor_tensor(h1[:, 2 * j:2 * j + 2, :], psX[:, j, :].rearrange("p (q d) -> p q d", q=2),
                                                        hb[:, 2 * j:2 * j + 2, :], ALU.add)
                                ins.then_inc(h1_done, 1)
                            dve.wait_ge(h1_done, 2 * i)
                            for q in range(QB):
                                ins = dve.bn_stats(stats2[:, q, :], h1[:, q, :])
                            link(ins)
                            dve.sem_inc(carry["dve"], 1)
                            for q in range(QB):
                                ins = dve.bn_aggr(mv2[:, q, :], stats2[:, q, :])
                            ins.then_inc(mv2_done, 1)
                        if cur:
                            for q in range(QB):
                                ins = dve.tensor_tensor(hb[:, q, :], h[:, q, :], bout_b[:, :], ALU.add)
                            ins.then_inc(k_hb, 1)
                        if nxt:
                            for j in range(2):
                                dve.wait_ge(lora_ready, 2 * (i + 1) + j + 1)
                                if j == 0:
                                    dve.wait_ge(rows_in, 2 * QB * 16 * (i + 2))
                                    if cur:
                                        dve.wait_ge(k_hb, i + 1)
                                dve.scalar_tensor_tensor(h[:, 2 * j:2 * j + 2, :], psX[:, 1 - j, :].rearrange("p (q d) -> p q d", q=2),
                                                         LORA_SCALE, emb_t[:, 2 * j:2 * j + 2, :], ALU.mult,
                                                         ALU.add).then_inc(h_done, 1)
                            dve.wait_ge(h_done, 2 * (i + 2))
                            link1 = Link(dve, k_ln1, 4, i + 1)
                            for q in range(QB):
                                ins = dve.bn_stats(stats1[:, q, :], h[:, q, :])
                            link1(ins)
                            dve.sem_inc(carry["dve"], 1)
                            for q in range(QB):
                                ins = dve.bn_aggr(mv1[:, q, :], stats1[:, q, :])
                            ins.then_inc(mv1_done, 1)
                        if cur:
                            dve.wait_ge(m_hi_done, i + 1)
                            if prev:
                                dve.wait_ge(m_out, 32 * i)
                            dve.tensor_tensor(m_lo[:, :], psX[0:2 * H, 1, :], m_hi[:, :].bitcast(F32),
                                              ALU.subtract).then_inc(m_lo_done, 1)
                        if prev:
                            dve.wait_ge(std2_done, i)
                            link(dve.reciprocal(rstd2[:, :], std2[:, :]))
                            dve.wait_ge(x2_out, 16 * (i - 1))
                            dve.wait_ge(x2_t_ready, KT * (i - 1))
                            dve.wait_ge(res_done, i - 1)
                            for q in range(QB):
                                dve.tensor_scalar(x2[:, q, :], h1[:, q, :], mv2[:, q, 0:1], rstd2[:, q:q + 1],
                                                  ALU.subtract, ALU.mult).then_inc(x2_done, 1)
                        if nxt:
                            dve.wait_ge(std1_done, i + 2)
                            link1(dve.reciprocal(rstd1[:, :], std1[:, :]))
                            if cur:
                                dve.wait_ge(xn_t_ready, KT * (i + 1))
                            for q in range(QB):
                                dve.tensor_scalar(xn[:, q, :], h[:, q, :], mv1[:, q, 0:1], rstd1[:, q:q + 1],
                                                  ALU.subtract, ALU.mult).then_inc(xn_done, 1)
                            for t in range(4):
                                dve.wait_ge(qk_hi_done, 4 * (i + 1) + t + 1)
                                if t == 0 and cur:
                                    dve.wait_ge(qk_out, 32 * (i + 1))
                                dve.scalar_tensor_tensor(qk_lo[:, t, :], psX[:, t % 2, :], bqk[:, t:t + 1],
                                                         qk_hi[:, t, :].bitcast(F32), ALU.add,
                                                         ALU.subtract).then_inc(qk_lo_done, 1)
                            dve.wait_ge(egate_done, i + 2)
                            link1(dve.tensor_scalar(egate1[:, :], egate[:, :], 1.0, None, ALU.add))
                            link1(dve.reciprocal(gate_new[:, :], egate1[:, :]))
                            link1.end()
                        if prev:
                            route_top(i)
                            route_rank(i)
                            link.end()
                        if nxt:
                            for j in range(2):
                                dve.wait_ge(v_ready, 2 * (i + 1) + j + 1)
                                for a in range(2):
                                    rows = slice(64 * a, 64 * (a + 1))
                                    dve.tensor_tensor(V[rows, 4 * j:4 * j + 4, :, 32 * a:32 * a + HD],
                                                      psX[rows, 1 - j, :].rearrange("p (k h d) -> p k h d", k=4, d=HD),
                                                      bv[rows, :, :].unsqueeze(1).to_broadcast([64, 4, PAIRS, HD]),
                                                      ALU.add).then_inc(v_done, 1)
                        if cur:
                            mixed(i, prev)
                    turns(dve, turn)

        attn_mem.close()
        with ExitStack() as mem:
            tmp = lambda name, shape, dt=F32: sb(mem, name, shape, dt)
            HT = E * HE
            CHUNKS = [(c, min(P, HT - c)) for c in range(0, HT, P)]
            tab_rows = tmp("tab_rows", [P, len(CHUNKS), P, 2], I32)
            tok_rows = tmp("tok_rows", [P, len(CHUNKS), P])
            tok_all = tmp("tok_all", [P, HT], I32)
            wt_all = tmp("wt_all", [P, HT])
            w1_raw = tmp("w1_raw", [P, KT, F])
            w2_raw = tmp("w2_raw", [P, FT, D])
            w1_hi = tmp("w1_hi", [P, KT, F], F32R)
            w1_lo = tmp("w1_lo", [P, KT, F], F32R)
            w2_hi = tmp("w2_hi", [P, FT, D], F32R)
            w2_lo = tmp("w2_lo", [P, FT, D], F32R)
            tok_in = tmp("tok_in", [P, 2], I32)
            tok_out = tmp("tok_out", [P, 2], I32)
            xg = tmp("xg", [P, 3, 2, D])
            xg_hi = tmp("xg_hi", [P, 3, KT, 2 * P], F32R)
            xg_lo = tmp("xg_lo", [P, 3, KT, 2 * P], F32R)
            act32 = tmp("act32", [P, 4, 2, 2 * P])
            h_hi = tmp("h_hi", [P, 3, FT, 2 * P], F32R)
            h_lo = tmp("h_lo", [P, 3, FT, 2 * P], F32R)
            out_t = tmp("out_t", [P, 3, 2, D])

            table_in, tok_rows_done, tab_t_ready, tab_done = sem("table_in"), sem("tok_rows_done"), sem("tab_t_ready"), sem("tab_done")
            w1_in, w2_in = sem("w1_in"), sem("w2_in")
            w1_hi_done, w1_lo_done, w2_hi_done, w2_lo_done = sem("w1_hi_done"), sem("w1_lo_done"), sem("w2_hi_done"), sem("w2_lo_done")
            tok_in_done, tok_out_done, xg_in = sem("tok_in_done"), sem("tok_out_done"), sem("xg_in")
            xg_t_ready, xg_hi_done, xg_lo_done = sem("xg_t_ready"), sem("xg_hi_done"), sem("xg_lo_done")
            up_ready, silu_done, h_lo_done = sem("up_ready"), sem("silu_done"), sem("h_lo_done")
            down_ready, out_done, y_added = sem("down_ready"), sem("out_done"), sem("y_added")

            TE = -(-HE // 2)
            LAST = HE - 2 * (TE - 1)
            TURNS = (TE - 2) // 2

            class Tile:
                def __init__(self, e, j, like):
                    last = like == TE - 1
                    self.e, self.first, self.second = e, like == 0, like == 1
                    self.buf = 2 if last and TE % 2 else like % 2
                    self.halves = LAST if last else 2
                    self.t = e * TE + j
                    self.h0 = e * HE + 2 * j

            def tiles(eng, step):
                def expert(e, first, last):
                    row = [None if first else Tile(e - 1, TE - 1, TE - 1)]
                    row += [Tile(e, j, j) for j in range(TE)]
                    row += [None if last else Tile(e + 1, 0, 0)]
                    looped = range(2, 2 * TURNS) if TURNS > 2 else range(0)
                    for j in range(TE):
                        if j not in looped:
                            step(row[j], row[j + 1], row[j + 2])
                        elif j == 2:
                            with eng.Fori(1, TURNS) as m:
                                for s in range(2):
                                    step(*(Tile(e, 2 * m + s + d, 2 + s + d) for d in (-1, 0, 1)))

                expert(0, True, False)
                with eng.Fori(1, E - 1) as e:
                    expert(e, False, False)
                expert(E - 1, False, True)
                step(Tile(E - 1, TE - 1, TE - 1), None, None)

            with nc.Block() as block:
                @block.sync
                def _(sp):
                    for c, (first, n) in enumerate(CHUNKS):
                        sp.dma_start(tab_rows[0:n, c, :, :],
                                     table[first * P:(first + n) * P, :].rearrange("(h p) w -> h p w", p=P)).then_inc(table_in, 16)

                    def weights(e):
                        sp.dma_start(w1_raw[:, :, :], w1[e].rearrange("(k p) f -> p k f", p=P)).then_inc(w1_in, 16)
                        if not isinstance(e, int):
                            sp.wait_ge(w2_hi_done, e)
                            sp.wait_ge(w2_lo_done, e)
                        sp.dma_start(w2_raw[:, :, :], w2[e].rearrange("(f p) d -> p f d", p=P)).then_inc(w2_in, 16)
                    weights(0)
                    with sp.Fori(1, E) as e:
                        sp.wait_ge(w1_hi_done, e)
                        sp.wait_ge(w1_lo_done, e)
                        weights(e)

                @block.gpsimd
                def _(pool):
                    def gather(tile):
                        pool.tensor_copy(tok_in[:, 0:tile.halves],
                                         tok_all[:, bass.ds(tile.h0, tile.halves)]).then_inc(tok_in_done, 1)
                        pool.wait_ge(tok_in_done, tile.t + 1)
                        pool.sem_inc(carry["pool"], 1)
                        for s in range(tile.halves):
                            pool.indirect_dma_start(out=xg[:, tile.buf, s, :], out_offset=None, in_=x2_rows[:, :],
                                                    in_offset=bass.IndirectOffsetOnAxis(ap=tok_in[:, s:s + 1], axis=0)).then_inc(xg_in, 16)

                    def step(prev, cur, nxt):
                        if nxt:
                            pool.wait_ge(xg_t_ready, cur.t + 1)
                            pool.sem_inc(carry["pool"], 1)
                            gather(nxt)
                        if prev:
                            if not (isinstance(prev.t, int) and prev.t == 0):
                                pool.wait_ge(y_added, 16 * prev.h0)
                                pool.sem_inc(carry["pool"], 1)
                            pool.tensor_copy(tok_out[:, 0:prev.halves],
                                             tok_all[:, bass.ds(prev.h0, prev.halves)]).then_inc(tok_out_done, 1)
                            pool.wait_ge(tok_out_done, prev.t + 1)
                            for s in range(prev.halves):
                                if s:
                                    pool.wait_ge(y_added, 16 * (prev.h0 + s))
                                pool.wait_ge(out_done, prev.h0 + s + 1)
                                pool.sem_inc(carry["pool"], 1)
                                pool.indirect_dma_start(out=y[:, :], in_=out_t[:, prev.buf, s, :], in_offset=None,
                                                        out_offset=bass.IndirectOffsetOnAxis(ap=tok_out[:, s:s + 1], axis=0),
                                                        compute_op=ALU.add).then_inc(y_added, 16)
                    pool.wait_ge(tab_done, 1)
                    gather(Tile(0, 0, 0))
                    tiles(pool, step)
                    pool.wait_ge(y_added, 16 * HT)

                @block.tensor
                def _(pe):
                    pe.wait_ge(tok_rows_done, 1)
                    for c, (first, n) in enumerate(CHUNKS):
                        pe.transpose(psX[:, 0, first:first + n], tok_rows[0:n, c, :], ident[0:n, 0:n])
                        last = pe.transpose(psX[:, 1, first:first + n], tab_rows[0:n, c, :, 1].bitcast(F32), ident[0:n, 0:n])
                    last.then_inc(tab_t_ready, 1)

                    def transposed(tile):
                        pe.wait_ge(xg_in, 16 * (tile.h0 + tile.halves))
                        if isinstance(tile.t, int) and tile.t == 0:
                            pe.wait_ge(tab_done, 1)
                        else:
                            pe.wait_ge(xg_lo_done, tile.t)
                        for k in range(KT):
                            for s in range(tile.halves):
                                last = pe.transpose(psX[:, 0, (2 * k + s) * P:(2 * k + s + 1) * P],
                                                    xg[:, tile.buf, s, k * P:(k + 1) * P], ident[:, :])
                        last.then_inc(xg_t_ready, 1)

                    def step(prev, cur, nxt):
                        if cur:
                            cols = cur.halves * P
                            pe.wait_ge(xg_lo_done, cur.t + 1)
                            if cur.first:
                                pe.wait_ge(w1_hi_done, cur.e + 1)
                                pe.wait_ge(w1_lo_done, cur.e + 1)
                            for f in range(FT):
                                if f % 2 == 0 and prev:
                                    pe.wait_ge(silu_done, 4 * prev.t + f // 2 + 1)
                                for k in range(KT):
                                    fs = slice(f * P, (f + 1) * P)
                                    for n, (w, x) in enumerate(((w1_hi, xg_hi), (w1_hi, xg_lo), (w1_lo, xg_hi))):
                                        last = pe.matmul(psS[:, f // 2, (f % 2) * 256:(f % 2) * 256 + cols], w[:, k, fs],
                                                         x[:, cur.buf, k, 0:cols], start=(k == 0 and n == 0),
                                                         stop=(k == KT - 1 and n == 2))
                                if f % 2:
                                    last.then_inc(up_ready, 1)
                        if nxt:
                            transposed(nxt)
                        if prev:
                            pe.wait_ge(h_lo_done, 4 * (prev.t + 1))
                            if prev.first:
                                pe.wait_ge(w2_hi_done, prev.e + 1)
                                pe.wait_ge(w2_lo_done, prev.e + 1)
                            for s in range(prev.halves):
                                if not (isinstance(prev.t, int) and prev.t == 0):
                                    pe.wait_ge(out_done, prev.h0)
                                for f in range(FT):
                                    ts = slice(s * P, (s + 1) * P)
                                    for n, (h_, w) in enumerate(((h_hi, w2_hi), (h_hi, w2_lo), (h_lo, w2_hi))):
                                        last = pe.matmul(psO[:, s, 0:D], h_[:, prev.buf, f, ts], w[:, f, :],
                                                         start=(f == 0 and n == 0), stop=(f == FT - 1 and n == 2))
                                last.then_inc(down_ready, 1)
                    transposed(Tile(0, 0, 0))
                    tiles(pe, step)

                @block.scalar
                def _(act):
                    def transposed(tile):
                        act.wait_ge(xg_t_ready, tile.t + 1)
                        cols = tile.halves * P
                        act.activation(xg_hi[:, tile.buf, :, 0:cols],
                                       psX[:, 0, :].rearrange("p (k c) -> p k c", k=KT)[:, :, 0:cols], ACT.Copy).then_inc(xg_hi_done, 1)

                    def step(prev, cur, nxt):
                        if cur and cur.first:
                            act.wait_ge(w1_in, 16 * (cur.e + 1))
                            if prev:
                                act.wait_ge(up_ready, 4 * cur.t)
                            act.activation(w1_hi[:, :, :], w1_raw[:, :, :], ACT.Copy).then_inc(w1_hi_done, 1)
                        if cur and cur.second:
                            act.wait_ge(w2_in, 16 * (cur.e + 1))
                            if not (isinstance(cur.e, int) and cur.e == 0):
                                act.wait_ge(down_ready, prev.h0)
                            act.activation(w2_hi[:, :, :], w2_raw[:, :, :], ACT.Copy).then_inc(w2_hi_done, 1)
                        if cur:
                            cols = cur.halves * P
                            for b in range(4):
                                act.wait_ge(up_ready, 4 * cur.t + b + 1)
                                if prev:
                                    act.wait_ge(h_lo_done, 4 * prev.t + b + 1)
                                src = psS[:, b, :].rearrange("p (f c) -> p f c", f=2)[:, :, 0:cols]
                                act.activation(act32[:, b, :, 0:cols], src, ACT.Silu)
                                act.activation(h_hi[:, cur.buf, 2 * b:2 * b + 2, 0:cols], src, ACT.Silu).then_inc(silu_done, 1)
                        if nxt:
                            transposed(nxt)
                    transposed(Tile(0, 0, 0))
                    tiles(act, step)

                @block.vector
                def _(dve):
                    dve.wait_ge(table_in, 16 * len(CHUNKS))
                    for c, (first, n) in enumerate(CHUNKS):
                        ins = dve.tensor_copy(tok_rows[0:n, c, :], tab_rows[0:n, c, :, 0])
                    ins.then_inc(tok_rows_done, 1)
                    dve.wait_ge(tab_t_ready, 1)
                    dve.tensor_copy(tok_all[:, :], psX[:, 0, 0:HT])
                    dve.tensor_copy(wt_all[:, :], psX[:, 1, 0:HT]).then_inc(tab_done, 1)

                    def transposed(tile):
                        dve.wait_ge(xg_hi_done, tile.t + 1)
                        cols = tile.halves * P
                        dve.tensor_tensor(xg_lo[:, tile.buf, :, 0:cols],
                                          psX[:, 0, :].rearrange("p (k c) -> p k c", k=KT)[:, :, 0:cols],
                                          xg_hi[:, tile.buf, :, 0:cols].bitcast(F32), ALU.subtract).then_inc(xg_lo_done, 1)

                    def step(prev, cur, nxt):
                        if cur and cur.first:
                            dve.wait_ge(w1_hi_done, cur.e + 1)
                            dve.tensor_tensor(w1_lo[:, :, :], w1_raw[:, :, :], w1_hi[:, :, :].bitcast(F32),
                                              ALU.subtract).then_inc(w1_lo_done, 1)
                        if cur and cur.second:
                            dve.wait_ge(w2_hi_done, cur.e + 1)
                            dve.tensor_tensor(w2_lo[:, :, :], w2_raw[:, :, :], w2_hi[:, :, :].bitcast(F32),
                                              ALU.subtract).then_inc(w2_lo_done, 1)
                        if cur:
                            cols = cur.halves * P
                            for b in range(4):
                                dve.wait_ge(silu_done, 4 * cur.t + b + 1)
                                dve.tensor_tensor(h_lo[:, cur.buf, 2 * b:2 * b + 2, 0:cols], act32[:, b, :, 0:cols],
                                                  h_hi[:, cur.buf, 2 * b:2 * b + 2, 0:cols].bitcast(F32),
                                                  ALU.subtract).then_inc(h_lo_done, 1)
                        if nxt:
                            transposed(nxt)
                        if prev:
                            for s in range(prev.halves):
                                dve.wait_ge(down_ready, prev.h0 + s + 1)
                                if s == 0 and not (isinstance(prev.t, int) and prev.t == 0):
                                    dve.wait_ge(y_added, 16 * prev.h0)
                                dve.tensor_scalar(out_t[:, prev.buf, s, :], psO[:, s, 0:D],
                                                  wt_all[:, bass.ds(prev.h0 + s, 1)], None, ALU.mult).then_inc(out_done, 1)
                    dve.wait_ge(tab_done, 1)
                    transposed(Tile(0, 0, 0))
                    tiles(dve, step)


_INS = ["x", "L0_tok_emb_weight", "L0_tok_lora_A", "L0_tok_lora_B", "L0_attn_Wqkv", "L0_attn_bqkv", "L0_attn_Wout",
        "L0_attn_bout", "L0_attn_Wg", "L0_attn_bg", "L0_ffn_router_w", "L0_ffn_w1", "L0_ffn_w2"]


def kernel(**inputs):
    import numpy as _np
    import concourse.bacc as _bacc
    from concourse import mybir as _mybir
    from concourse.bass_utils import run_bass_kernel_spmd as _run

    nc = _bacc.Bacc("TRN2", target_bir_lowering=False, num_devices=1)
    arrays, args = {}, []
    for name in _INS:
        a = _np.ascontiguousarray(inputs[name])
        arrays[f"in_{name}"] = a
        args.append(nc.dram_tensor(f"in_{name}", a.shape, _mybir.dt.from_np(a.dtype), kind="ExternalInput").ap())
    seqs = inputs["x"].shape[0]
    args.append(nc.dram_tensor("out_y", [seqs * T + P, D], _mybir.dt.float32, kind="ExternalOutput").ap())
    build(nc, *args)
    r = _run(nc, [arrays], core_ids=[0])
    return r.results[0]["out_y"][:seqs * T].reshape(seqs, T, D)
```

```python
from contextlib import ExitStack

import numpy as np
import concourse.bass as bass
from concourse import mybir

F32 = mybir.dt.float32
F32R = mybir.dt.float32r
BF16 = mybir.dt.bfloat16
I32 = mybir.dt.int32
U32 = mybir.dt.uint32
ALU = mybir.AluOpType
ACT = mybir.ActivationFunctionType
AX = mybir.AxisListType

P = 128
D = 256
KT = D // P
H = 16
HD = D // H
PAIRS = H // 2
DUOS = PAIRS // 2
T = 512
QB = T // P
KB = T // 64
R = 16
E = 8
F = 1024
FT = F // P
EPS = 1e-5
LORA_SCALE = 2.0
SCALE = HD ** -0.5
MASKED = -1e30
VG = 8
M_JOBS = PAIRS * (QB + 1)
E_JOBS = PAIRS * (KB // 2 + 1)


class Link:

    def __init__(self, eng, sem, n, turn):
        self.eng, self.sem, self.n, self.turn, self.k = eng, sem, n, turn, 0

    def __call__(self, ins):
        self.k += 1
        ins.then_inc(self.sem, 1)
        self.eng.wait_ge(self.sem, self.n * self.turn + self.k)

    def end(self):
        assert self.k == self.n, (self.k, self.n)


def build(nc, x, emb, lora_a, lora_b, wqkv, bqkv, wout, bout, wg, bg, rw, w1, w2, y):
    SEQ = x.shape[0]
    N = SEQ * T
    VOCAB = emb.shape[0]
    TOKT = N // P
    CAP = int(1.25 * N * 2 / E) + 1
    HE = -(-CAP // P)
    STRIDE = HE * P
    SLOTS = E * STRIDE
    GT = -(-VOCAB // (VG * P)) * P
    STEPS = GT // P
    GP = PAIRS // 2
    FAR = float(1 << 20)

    lora_rows = nc.dram_tensor("lora_rows", [VG * GT, R], F32, kind="Internal").ap()
    qk_scr = nc.dram_tensor("qk_scr", [2, 2 * D, T], F32, kind="Internal").ap()
    m_scr = nc.dram_tensor("m_scr", [2, 2, 2, PAIRS, T], F32, kind="Internal").ap()
    x2_rows = nc.dram_tensor("x2_rows", [N + P, D], F32, kind="Internal").ap()
    table = nc.dram_tensor("slot_table", [SLOTS, 2], I32, kind="Internal").ap()

    outer = ExitStack()
    with outer:
        def sb(ctx, name, shape, dt=F32):
            return ctx.enter_context(nc.sbuf_tensor(name, shape, dt))

        def sem(name):
            return outer.enter_context(nc.semaphore(name))

        psS = outer.enter_context(nc.psum_tensor("psS", [P, 4, 512], F32))
        psO = outer.enter_context(nc.psum_tensor("psO", [P, 2, 512], F32))
        psX = outer.enter_context(nc.psum_tensor("psX", [P, 2, 512], F32))

        ident = sb(outer, "ident", [P, P])
        counts = sb(outer, "counts", [P, E], BF16)
        onesb = sb(outer, "onesb", [P, P], BF16)

        attn_mem = ExitStack()
        outer.enter_context(attn_mem)
        keep = lambda name, shape, dt=F32: sb(attn_mem, name, shape, dt)
        identb = keep("identb", [P, P], BF16)
        upper = keep("upper", [P, P], BF16)
        ids = keep("ids", [P, TOKT + QB], I32)
        mask_q = keep("mask_q", [P, 4, 2, 64], BF16)
        mask_k = keep("mask_k", [P, 2, 2, 64], BF16)
        wv_sb = keep("wv_sb", [P, KT, D])
        wout_sb = keep("wout_sb", [P, KT, D])
        wg_b = keep("wg_b", [P, D])
        rw_t = keep("rw_t", [P, KT, E])
        lb_t = keep("lb_t", [R, D])
        wqk = keep("wqk", [P, KT, 4, P])
        bqk = keep("bqk", [P, 4])
        bv = keep("bv", [P, PAIRS, HD])
        bout_b = keep("bout_b", [P, D])
        neg_bg = keep("neg_bg", [P, 1])
        eps_b = keep("eps_b", [P, 1])
        iota8 = keep("iota8", [P, E])
        tokid = keep("tokid", [P, QB])
        Q = keep("Q", [P, PAIRS, T], F32R)
        K = keep("K", [P, PAIRS, KB, 2, 64], F32R)
        KG = keep("KG", [P, PAIRS, 2, 64], F32R)
        V = keep("V", [P, KB, PAIRS, 64])

        with ExitStack() as mem:
            tmp = lambda name, shape, dt=F32: sb(mem, name, shape, dt)
            la_src = tmp("la_src", [P, GT])
            la_dst = tmp("la_dst", [P, VG, STEPS, R])
            wqk_raw = tmp("wqk_raw", [P, KT, 2 * D])
            ids_rows = tmp("ids_rows", [TOKT, P], I32)
            ids_f = tmp("ids_f", [TOKT, P])
            rw_rows = tmp("rw_rows", [E, D])
            bqk_rows = tmp("bqk_rows", [4, P])
            lb_rows = tmp("lb_rows", [P, KT, R])
            bg_b = tmp("bg_b", [P, 1])
            rowsel = tmp("rowsel", [P, 2, 2])
            tab_i = tmp("tab_i", [P, SLOTS // P], I32)
            tab = tmp("tab", [P, SLOTS // P, 2], I32)
            zpad = tmp("zpad", [P, D])
            weights_in, small_in, lora_in = sem("weights_in"), sem("small_in"), sem("lora_in")
            pool_base, pool_sel = sem("pool_base"), sem("pool_sel")
            dve_base, dve_made = sem("dve_base"), sem("dve_made")
            pe_small, dve_small = sem("pe_small"), sem("dve_small")
            step_ready, step_copied = sem("step_ready"), sem("step_copied")
            scratch_out = sem("scratch_out")
            POOL_SEL = 11
            chunks = [(s, min(4, STEPS - s)) for s in range(0, STEPS, 4)]

            with nc.Block() as block:
                @block.sync
                def _(sp):
                    sp.dma_start(ids_rows[:, :], x.rearrange("s (c p) -> (s c) p", p=P)).then_inc(small_in, 16)
                    sp.dma_start(rw_rows[:, :], rw).then_inc(small_in, 16)
                    sp.dma_start(lb_rows[:, :, :], lora_b.rearrange("(k p) r -> p k r", p=P)).then_inc(small_in, 16)
                    sp.dma_start(bg_b[:, :], bg.rearrange("(a n) -> a n", a=1).to_broadcast([P, 1])).then_inc(small_in, 16)
                    sp.wait_ge(dve_base, 1)
                    for g in range(VG):
                        n = min(GT, VOCAB - g * GT)
                        sp.dma_start(la_src[R * g:R * (g + 1), 0:n], lora_a[:, g * GT:g * GT + n]).then_inc(lora_in, 16)
                    sp.wait_ge(dve_made, 3)
                    sp.dma_start(table.rearrange("(p j) w -> p j w", p=P), tab[:, :, :]).then_inc(scratch_out, 16)
                    sp.dma_start(x2_rows[N:N + P, :], zpad[:, :]).then_inc(scratch_out, 16)
                    sp.dma_start(y[N:N + P, :], zpad[:, :]).then_inc(scratch_out, 16)
                    sp.wait_ge(step_copied, len(chunks))
                    for g in range(VG):
                        sp.dma_start(lora_rows[g * GT:(g + 1) * GT, :].rearrange("(p s) r -> p s r", p=P),
                                     la_dst[:, g, :, :]).then_inc(scratch_out, 16)
                    sp.wait_ge(scratch_out, 16 * (3 + VG))

                @block.scalar
                def _(act):
                    wqkv_k = wqkv.rearrange("(k p) n -> p k n", p=P)
                    act.dma_start(wqk_raw[:, :, :], wqkv_k[:, :, 0:2 * D]).then_inc(weights_in, 16)
                    act.dma_start(wv_sb[:, :, :], wqkv_k[:, :, 2 * D:3 * D]).then_inc(weights_in, 16)
                    act.dma_start(wout_sb[:, :, :], wout.rearrange("(k p) n -> p k n", p=P)).then_inc(weights_in, 16)
                    act.dma_start(wg_b[:, :], wg.rearrange("d n -> n d").to_broadcast([P, D])).then_inc(weights_in, 16)
                    for s in range(2):
                        for a in range(2):
                            act.dma_start(bqk_rows[2 * s + a:2 * s + a + 1, :].rearrange("o (d h) -> o d h", d=HD),
                                          bqkv[s * D:(s + 1) * D].rearrange("(o h a d) -> a o d h", o=1, a=2, d=HD)[a],
                                          allow_slow_non_contiguous=True).then_inc(weights_in, 16)
                    bvv = bqkv[2 * D:3 * D].rearrange("(o p a d) -> o a p d", o=1, a=2, d=HD)
                    for a in range(2):
                        act.dma_start(bv[64 * a:64 * (a + 1), :, :],
                                      bvv[:, a, :, :].to_broadcast([64, PAIRS, HD])).then_inc(weights_in, 16)
                    act.dma_start(bout_b[:, :],
                                  bout.rearrange("(a n) -> a n", a=1).to_broadcast([P, D])).then_inc(weights_in, 16)
                    act.wait_ge(weights_in, 16 * 11)

                @block.gpsimd
                def _(pool):
                    pool.iota(iota8[:, :], [[1, E]], base=0, channel_multiplier=0,
                              allow_small_or_imprecise_dtypes=True).then_inc(pool_base, 1)
                    pool.wait_ge(pool_base, 1)
                    pool.iota(tokid[:, :], [[P, QB]], base=0, channel_multiplier=1,
                              allow_small_or_imprecise_dtypes=True).then_inc(pool_base, 1)
                    pool.wait_ge(pool_base, 2)
                    pool.iota(tab_i[:, :], [[1, SLOTS // P]], base=0, channel_multiplier=SLOTS // P).then_inc(pool_base, 1)
                    pool.wait_ge(dve_base, 2)
                    made = [0]

                    def select(ap, op, fill, base, pattern, per_row):
                        pool.affine_select(out=ap, in_=ap, compare_op=op, fill=fill, base=base, pattern=pattern,
                                           channel_multiplier=per_row).then_inc(pool_sel, 1)
                        made[0] += 1
                        pool.wait_ge(pool_sel, made[0])

                    for m in (ident, identb):
                        select(m[:, :], ALU.not_equal, 1.0, 0, [[-1, P]], 1)
                    select(upper[:, :], ALU.is_gt, 0.0, 0, [[1, P]], -1)
                    select(mask_q[:, :, :, :], ALU.is_ge, MASKED, 0, [[64, 4], [0, 2], [1, 64]], -1)
                    select(mask_q[:, :, :, :], ALU.is_ge, MASKED, P, [[-64, 4], [0, 2], [-1, 64]], 1)
                    for a in range(2):
                        rows = slice(64 * a, 64 * (a + 1))
                        select(mask_k[rows, :, 0, :], ALU.is_ge, MASKED, 0, [[0, 2], [1, 64]], -1)
                        select(mask_k[rows, :, 1, :], ALU.is_ge, MASKED, 0, [[0, 2], [-1, 64]], 1)
                    for first in (48, 50):
                        select(rowsel[:, :, :], ALU.not_equal, 1.0, -first, [[-1, 2], [-64, 2]], 1)
                    assert made[0] == POOL_SEL

                @block.vector
                def _(dve):
                    dve.memset(la_src[P - 32:P, VOCAB - (VG - 1) * GT:GT], 0.0).then_inc(dve_base, 1)
                    for m in (ident, identb):
                        dve.memset(m[:, :], 0.0)
                    dve.memset(upper[:, :], 1.0)
                    dve.memset(onesb[:, :], 1.0)
                    dve.memset(mask_q[:, :, :, :], 0.0)
                    dve.memset(mask_k[:, :, :, :], 0.0)
                    dve.memset(rowsel[:, :, :], 0.0).then_inc(dve_base, 1)
                    dve.memset(zpad[:, :], 0.0)
                    dve.memset(tab[:, :, :], 0)
                    dve.memset(ids[:, TOKT:TOKT + QB], 0)
                    dve.memset(counts[:, :], 0.0)
                    dve.memset(eps_b[:, :], EPS)
                    dve.memset(Q[:, :, :].bitcast(F32), 0.0)
                    dve.memset(KG[:, :, :, :].bitcast(F32), 0.0)
                    dve.memset(K[:, :, :, :, :].bitcast(F32), 0.0)
                    dve.memset(V[:, :, :, :], 0.0).then_inc(dve_made, 1)
                    dve.wait_ge(pool_base, 3)
                    dve.tensor_scalar(tab_i[:, :], tab_i[:, :], P - 1, None, ALU.bitwise_and).then_inc(dve_made, 1)
                    dve.wait_ge(dve_made, 2)
                    dve.tensor_scalar(tab[:, :, 0], tab_i[:, :], float(N), None, ALU.add).then_inc(dve_made, 1)
                    dve.memset(V[0:64, :, :, 16:32], 1.0)
                    dve.memset(V[64:P, :, :, 48:64], 1.0)
                    dve.wait_ge(pool_sel, POOL_SEL)
                    for a in range(2):
                        dve.tensor_scalar(K[:, :, :, a, :], K[:, :, :, a, :].bitcast(F32), rowsel[:, 0, a:a + 1], None, ALU.add)
                        dve.tensor_scalar(KG[:, :, a, :], KG[:, :, a, :].bitcast(F32), rowsel[:, 1, a:a + 1], None, ALU.add)
                    dve.wait_ge(weights_in, 16 * 11)
                    for k in range(KT):
                        for s in range(2):
                            dve.tensor_copy(wqk[:, k, 2 * s:2 * s + 2, :].rearrange("p a (d h) -> p a d h", d=HD),
                                            wqk_raw[:, k, s * D:(s + 1) * D].rearrange("p (h a d) -> p a d h", a=2, d=HD))
                    dve.wait_ge(small_in, 64)
                    dve.tensor_scalar(neg_bg[:, :], bg_b[:, :], -1.0, None, ALU.mult)
                    dve.tensor_copy(ids_f[:, :], ids_rows[:, :]).then_inc(dve_small, 1)
                    dve.wait_ge(pe_small, 1)
                    dve.tensor_copy(ids[:, 0:TOKT], psO[:, 0, 0:TOKT])
                    dve.tensor_copy(rw_t[:, :, :], psO[:, 0, 256:256 + KT * E].rearrange("p (k e) -> p k e", k=KT))
                    dve.tensor_copy(lb_t[:, :], psO[0:R, 1, 0:D])
                    dve.tensor_copy(bqk[:, :], psO[:, 0, 300:304])
                    for c, (s, n) in enumerate(chunks):
                        dve.wait_ge(step_ready, c + 1)
                        dve.tensor_copy(la_dst[:, :, s:s + n, :],
                                        psX[:, c % 2, 0:n * P].rearrange("p (s g r) -> p g s r", s=n, g=VG)).then_inc(step_copied, 1)

                @block.tensor
                def _(pe):
                    pe.wait_ge(pool_sel, 1)
                    pe.wait_ge(small_in, 64)
                    pe.wait_ge(dve_small, 1)
                    pe.transpose(psO[:, 0, 0:TOKT], ids_f[:, :], ident[0:TOKT, 0:TOKT])
                    for k in range(KT):
                        pe.transpose(psO[:, 0, 256 + k * E:256 + (k + 1) * E], rw_rows[:, k * P:(k + 1) * P], ident[0:E, 0:E])
                    for k in range(KT):
                        pe.transpose(psO[0:R, 1, k * P:(k + 1) * P], lb_rows[:, k, :], ident[:, :])
                    pe.wait_ge(weights_in, 16 * 11)
                    pe.transpose(psO[:, 0, 300:304], bqk_rows[:, :], ident[0:4, 0:4]).then_inc(pe_small, 1)
                    pe.wait_ge(lora_in, 16 * VG)
                    for c, (s, n) in enumerate(chunks):
                        if c >= 2:
                            pe.wait_ge(step_copied, c - 1)
                        for j in range(n):
                            last = pe.transpose(psX[:, c % 2, j * P:(j + 1) * P],
                                                la_src[:, s + j:s + j + (P - 1) * STEPS + 1:STEPS], ident[:, :])
                        last.then_inc(step_ready, 1)

        with ExitStack() as mem:
            tmp = lambda name, shape, dt=F32: sb(mem, name, shape, dt)
            id_cur = tmp("id_cur", [P, QB], I32)
            emb_t = tmp("emb_t", [P, QB, D])
            la = tmp("la", [P, QB, R])
            la_t = tmp("la_t", [R, T])
            h = tmp("h", [P, QB, D])
            hb = tmp("hb", [P, QB, D])
            stats1 = tmp("stats1", [P, QB, 6])
            mv1 = tmp("mv1", [P, QB, 2])
            std1 = tmp("std1", [P, QB])
            rstd1 = tmp("rstd1", [P, QB])
            xn = tmp("xn", [P, QB, D])
            xn_t = tmp("xn_t", [P, KT, T])
            xn_wg = tmp("xn_wg", [P, QB, D])
            zgate = tmp("zgate", [P, QB])
            egate = tmp("egate", [P, QB])
            egate1 = tmp("egate1", [P, QB])
            gate_new = tmp("gate_new", [P, QB])
            gates = tmp("gates", [P, 2, QB])
            qk_hi = tmp("qk_hi", [P, 4, T], F32R)
            qk_lo = tmp("qk_lo", [P, 4, T], F32R)
            negm = tmp("negm", [P, QB, 2, 2, PAIRS])
            m_hl = tmp("m_hl", [H, 2, T], F32R)
            pl = tmp("pl", [P, 4, KB // 2, 384])
            pg = tmp("pg", [P, 4, T])
            o_t = tmp("o_t", [P, 2, DUOS, T])
            rsum = tmp("rsum", [P, 2, H])
            coef = tmp("coef", [P, 2, H])
            mix = tmp("mix", [P, 2, 2, H, HD])
            attn = tmp("attn", [P, QB, D])
            attn_t = tmp("attn_t", [P, KT, T])
            h1 = tmp("h1", [P, QB, D])
            stats2 = tmp("stats2", [P, QB, 6])
            mv2 = tmp("mv2", [P, QB, 2])
            std2 = tmp("std2", [P, QB])
            rstd2 = tmp("rstd2", [P, QB])
            x2 = tmp("x2", [P, QB, D])
            x2_t = tmp("x2_t", [P, KT, T])
            logit = tmp("logit", [P, QB, E])
            top = tmp("top", [P, QB, 8])
            top_i = tmp("top_i", [P, QB, 8], U32)
            top_f = tmp("top_f", [P, QB, 2])
            gap = tmp("gap", [P, QB])
            egap = tmp("egap", [P, QB])
            egap1 = tmp("egap1", [P, QB])
            prob = tmp("prob", [P, QB, 2])
            onehot = tmp("onehot", [P, QB, 2, E])
            chosen = tmp("chosen", [P, QB, E], BF16)
            before = tmp("before", [P, QB + 1, E], BF16)
            ahead = tmp("ahead", [P, QB, E])
            picked = tmp("picked", [P, QB, 2, E])
            rank = tmp("rank", [P, QB, 2])
            over = tmp("over", [P, QB, 2])
            slot = tmp("slot", [P, QB, 2])
            slot_i = tmp("slot_i", [P, QB, 2], I32)
            entry = tmp("entry", [P, QB, 2, 2], I32)

            id_ready, rows_in = sem("id_ready"), sem("rows_in")
            la_t_ready, la_t_done, lora_ready = sem("la_t_ready"), sem("la_t_done"), sem("lora_ready")
            h_done, mv1_done, std1_done, xn_done = sem("h_done"), sem("mv1_done"), sem("std1_done"), sem("xn_done")
            xn_t_ready, xn_t_done = sem("xn_t_ready"), sem("xn_t_done")
            qk_ready, qk_hi_done, qk_lo_done = sem("qk_ready"), sem("qk_hi_done"), sem("qk_lo_done")
            gate_ready, egate_done = sem("gate_ready"), sem("egate_done")
            v_ready, v_done = sem("v_ready"), sem("v_done")
            qk_out = sem("qk_out")
            half_in = [sem("half0_in"), sem("half1_in")]
            s_ready, max_done = sem("s_ready"), sem("max_done")
            m_t_ready, m_hi_done, m_lo_done = sem("m_t_ready"), sem("m_hi_done"), sem("m_lo_done")
            m_out, m_in = sem("m_out"), sem("m_in")
            st_ready, exp_done = sem("st_ready"), sem("exp_done")
            ol_ready, og_ready, ol_done, og_done = sem("ol_ready"), sem("og_ready"), sem("ol_done"), sem("og_done")
            o_ready, o_read, attn_done = sem("o_ready"), sem("o_read"), sem("attn_done")
            attn_t_ready, attn_t_done = sem("attn_t_ready"), sem("attn_t_done")
            wout_ready, h1_done = sem("wout_ready"), sem("h1_done")
            mv2_done, std2_done, x2_done = sem("mv2_done"), sem("std2_done"), sem("x2_done")
            x2_t_ready, x2_t_done = sem("x2_t_ready"), sem("x2_t_done")
            logit_ready, logit_done, gap_done, egap_done = sem("logit_ready"), sem("logit_done"), sem("gap_done"), sem("egap_done")
            chosen_done, ahead_ready, ahead_done, entry_done = sem("chosen_done"), sem("ahead_ready"), sem("ahead_done"), sem("entry_done")
            res_done, y_out, x2_out, entry_out = sem("res_done"), sem("y_out"), sem("x2_out"), sem("entry_out")
            k_ln1, k_ln2, k_top, k_rank, k_mix = (sem("k_ln1"), sem("k_ln2"), sem("k_top"), sem("k_rank"),
                                                  sem("k_mix"))
            hb_done, xn_wg_done = sem("hb_done"), sem("xn_wg_done")
            HALF_DMAS = 20 * 16
            carry = {"sp": sem("sp_carry"), "pool": sem("pool_carry"), "dve": sem("dve_carry")}

            def turns(eng, turn):
                turn(-1, False, False, True)
                turn(0, False, True, True)
                turn(1, True, True, True)
                with eng.Fori(2, SEQ - 1) as i:
                    turn(i, True, True, True)
                turn(SEQ - 1, True, True, False)
                turn(SEQ, True, False, False)

            def order(prev, cur, nxt):
                E_HALF, M_HALF, DUO_JOBS = E_JOBS // 2, M_JOBS // 2, E_JOBS // DUOS
                maxima = iter(range(M_HALF, M_JOBS) if cur else ())
                next_maxima = iter(range(M_HALF) if nxt else ())

                def some(tiles, n, s):
                    for _ in range(n):
                        for tile in tiles:
                            yield "max", (s, tile)
                            break

                for stage, arg in START:
                    if stage == "max":
                        yield from some(maxima, arg, 0)
                    elif {"prev": prev, "cur": cur, "nxt": nxt}[OF[stage]]:
                        yield stage, arg
                for n in range(E_JOBS):
                    if cur:
                        yield "exp", n
                        if n >= DUO_JOBS and n % DUO_JOBS <= KB:
                            yield "out", (n // DUO_JOBS - 1, n % DUO_JOBS)
                        if n == M_ROWS:
                            yield "m_rows", 1
                    yield from some(maxima, 1, 0)
                    if n >= NEXT_MAX:
                        yield from some(next_maxima, 1, 1)
                    if prev and n in PREV_AT:
                        yield PREV_AT[n]
                    if nxt and n in NXT_AT:
                        yield NXT_AT[n]
                for c in range(KB + 1):
                    if cur:
                        yield "out", (DUOS - 1, c)
                    yield from some(next_maxima, OUT_MAX[c], 1)
                for q in range(QB):
                    if cur:
                        yield "mix", q
                    yield from some(next_maxima, MIX_MAX[q], 1)
                yield from some(next_maxima, M_HALF, 1)

            OF = {"m_rows": "cur", "values": "cur", "keep_h": "cur", "attn_t": "prev", "project": "prev",
                  "embed": "nxt", "norm1": "nxt"}
            START = (("m_rows", 0), ("attn_t", None), ("max", 1), ("values", 0), ("values", 1), ("max", 2),
                     ("project", 0), ("max", 1), ("project", 1), ("keep_h", None), ("max", 2), ("embed", None),
                     ("max", 2))
            M_ROWS, NEXT_MAX = 13, 35
            OUT_MAX, MIX_MAX = (0, 0, 2, 0, 0, 0, 1, 0, 2), (3, 3, 3, 3)
            PREV_AT = {19: ("norm2", None), 21: ("x2_t", None), 24: ("router", None), 26: ("weights", None),
                      28: ("ahead", None)}
            NXT_AT = {0: ("norm1", None), 6: ("xn_t", None), 8: ("qk", 0), 10: ("qk", 1), 14: ("qk", 2), 16: ("qk", 3),
                      19: ("gate", None)}

            def keys_of(qb):
                lo, hi = max(0, 2 * qb - 1), min(KB, 2 * qb + 3)
                return lo, hi, lo - (2 * qb - 1)

            class Bank:
                def __init__(self):
                    self.last = [None, None]

                def take(self, pe, b, i, signal, per, k, rel):
                    if self.last[b] is not None:
                        s, p_, k_, r_ = self.last[b]
                        pe.wait_ge(s, p_ * (i + r_) + k_)
                    self.last[b] = (signal, per, k, rel)

                def next_turn(self):
                    self.last = [x and (*x[:3], x[3] - 1) for x in self.last]

            with nc.Block() as block:
                @block.gpsimd
                def _(pool):
                    def gather(s):
                        pool.tensor_copy(id_cur[:, :], ids[:, bass.ts(s, QB)]).then_inc(id_ready, 1)
                        pool.wait_ge(id_ready, s + 1)
                        pool.sem_inc(carry["pool"], 1)
                        for q in range(QB):
                            at = bass.IndirectOffsetOnAxis(ap=id_cur[:, q:q + 1], axis=0)
                            pool.indirect_dma_start(out=la[:, q, :], out_offset=None, in_=lora_rows[:, :],
                                                    in_offset=at).then_inc(rows_in, 16)
                            pool.indirect_dma_start(out=emb_t[:, q, :], out_offset=None, in_=emb[:, :],
                                                    in_offset=at).then_inc(rows_in, 16)

                    def turn(i, prev, cur, nxt):
                        for stage, arg in order(prev, cur, nxt):
                            if stage == "ahead":
                                pool.wait_ge(entry_done, i)
                                pool.sem_inc(carry["pool"], 1)
                                for q in range(QB):
                                    for k in range(2):
                                        pool.indirect_dma_start(
                                            out=table[:, :], in_=entry[:, q, k, :], in_offset=None,
                                            out_offset=bass.IndirectOffsetOnAxis(ap=slot_i[:, q, k:k + 1], axis=0),
                                            bounds_check=SLOTS - 1, oob_is_err=False).then_inc(entry_out, 16)
                            if stage == "mix":
                                if arg == 0 and prev:
                                    pool.wait_ge(attn_t_ready, KT * i)
                                pool.wait_ge(o_read, QB * i + arg + 1)
                                pool.tensor_tensor(attn[:, arg, :].rearrange("p (h d) -> p h d", h=H), mix[:, arg % 2, 0, :, :],
                                                   mix[:, arg % 2, 1, :, :], ALU.add).then_inc(attn_done, 1)
                            if stage == "keep_h":
                                if prev:
                                    pool.wait_ge(h1_done, 2 * i)
                                pool.tensor_tensor(hb[:, :, :], h[:, :, :], bout_b[:, :].unsqueeze(1).to_broadcast([P, QB, D]),
                                                   ALU.add).then_inc(hb_done, 1)
                            if stage == "embed":
                                pool.wait_ge(rows_in, 2 * QB * 16 * (i + 2))
                                pool.wait_ge(h_done, 2 * (i + 2))
                                pool.sem_inc(carry["pool"], 1)
                                gather(i + 2)
                            if stage == "norm1":
                                pool.wait_ge(xn_done, QB * (i + 2))
                                if cur:
                                    pool.wait_ge(gate_ready, i + 1)
                                pool.tensor_tensor(xn_wg[:, :, :], xn[:, :, :], wg_b[:, :].unsqueeze(1).to_broadcast([P, QB, D]),
                                                   ALU.mult).then_inc(xn_wg_done, 1)
                            if stage == "norm2":
                                pool.wait_ge(x2_done, QB * i)
                                pool.tensor_tensor(h1[:, :, :], h1[:, :, :], x2[:, :, :], ALU.add).then_inc(res_done, 1)
                    gather(0)
                    turns(pool, turn)
                    pool.wait_ge(rows_in, 2 * QB * 16 * (SEQ + 1))
                    pool.wait_ge(entry_out, 2 * QB * 16 * SEQ)

                @block.sync
                def _(sp):
                    y_seq = y[0:N, :].rearrange("(s q p) d -> s p q d", q=QB, p=P)
                    zeros = x2_rows[N:N + 4 * T // D, :].rearrange("(r c) d -> r (c d)", r=4)
                    x2_seq = x2_rows[0:N, :].rearrange("(s q p) d -> s p q d", q=QB, p=P)

                    def m_rows(i, half, prev):
                        done, pairs = 2 * i + half, slice(GP * half, GP * (half + 1))
                        sp.wait_ge(m_hi_done, done + 1)
                        sp.sem_inc(carry["sp"], 1)
                        sp.wait_ge(m_lo_done, done + 1)
                        sp.sem_inc(carry["sp"], 1)
                        if prev:
                            sp.wait_ge(m_in, 32 * done)
                            sp.sem_inc(carry["sp"], 1)
                        sp.dma_start(m_scr[half].rearrange("l k h t -> (k h) l t"), m_hl[:, :, :].bitcast(F32)).then_inc(m_out, 16)
                        sp.wait_ge(m_out, 16 * (done + 1))
                        for a in range(2):
                            sp.dma_start(Q[64 * a + 48:64 * a + 52, pairs, :].bitcast(F32),
                                         m_scr[half].rearrange("l k (p a) t -> a (l k) p t", a=2)[a]).then_inc(m_in, 16)

                    def load_half(i, g, cur):
                        if cur:
                            sp.wait_ge(st_ready, E_JOBS * i + E_JOBS // 2 * (g + 1))
                        half = slice(GP * g, GP * (g + 1))
                        src = qk_scr.rearrange("l (s a d p) t -> s l a d p t", s=2, a=2, d=HD)
                        for a in range(2):
                            for j, (lq, lk) in enumerate(((0, 0), (1, 0), (0, 1))):
                                rows = slice(64 * a + HD * j, 64 * a + HD * (j + 1))
                                sp.dma_start(Q[rows, half, :].bitcast(F32), src[0, lq, a][:, half]).then_inc(half_in[g], 16)
                                keys = src[1, lk, a][:, half]
                                sp.dma_start(K[rows, half, :, a, :].rearrange("d p k c -> d (p k) c").bitcast(F32),
                                             keys.rearrange("d p (k c) -> d (p k) c", c=64)).then_inc(half_in[g], 16)
                                sp.dma_start(KG[rows, half, a, :].bitcast(F32), keys[:, :, 0:64]).then_inc(half_in[g], 16)
                            sp.dma_start(Q[64 * a + 48:64 * a + 52, half, :].bitcast(F32), zeros.unsqueeze(1).to_broadcast([4, GP, T])).then_inc(half_in[g], 16)

                    def turn(i, prev, cur, nxt):
                        if cur:
                            m_rows(i, 0, prev)
                            m_rows(i, 1, prev)
                        if nxt:
                            sp.wait_ge(qk_hi_done, 4 * (i + 2))
                            sp.sem_inc(carry["sp"], 1)
                            sp.wait_ge(qk_lo_done, 4 * (i + 2))
                            sp.sem_inc(carry["sp"], 1)
                            if cur:
                                for g in range(2):
                                    sp.wait_ge(half_in[g], HALF_DMAS * (i + 1))
                            for l, rows in enumerate((qk_hi, qk_lo)):
                                sp.dma_start(qk_scr[l].rearrange("(g p) t -> p g t", p=P),
                                             rows[:, :, :].bitcast(F32)).then_inc(qk_out, 16)
                            sp.wait_ge(qk_out, 32 * (i + 2))
                            sp.sem_inc(carry["sp"], 1)
                        if nxt:
                            load_half(i, 0, cur)
                        if prev:
                            sp.wait_ge(x2_done, QB * i)
                            sp.dma_start(x2_seq[i - 1], x2[:, :, :]).then_inc(x2_out, 16)
                            sp.wait_ge(res_done, i)
                            sp.dma_start(y_seq[i - 1], h1[:, :, :]).then_inc(y_out, 16)
                        if nxt:
                            load_half(i, 1, cur)
                    turns(sp, turn)
                    sp.wait_ge(x2_out, 16 * SEQ)
                    sp.wait_ge(y_out, 16 * SEQ)

                @block.tensor
                def _(pe):
                    bank = Bank()

                    def max_tile(s, n):
                        pr, q = divmod(n, QB + 1)
                        if n % (M_JOBS // 2) == 0:
                            half = n // (M_JOBS // 2)
                            pe.wait_ge(half_in[half], HALF_DMAS * (s + 1))
                        if not (isinstance(s, int) and s == 0 and n < 2):
                            pe.wait_ge(max_done, M_JOBS * s + n - 1)
                        out = psS[:, 2 + n % 2, :]
                        if q < QB:
                            lo, hi, w = keys_of(q)
                            cols = (hi - lo) * P
                            pe.matmul(out[:, 0:cols], identb[:, :], mask_q[:, w:w + hi - lo, :, :],
                                      start=True, stop=False)
                            last = pe.matmul(out[:, 0:cols], Q[:, pr, q * P:(q + 1) * P], K[:, pr, lo:hi, :, :],
                                             start=False, stop=True)
                        else:
                            for b in range(QB):
                                last = pe.matmul(out[:, b * P:(b + 1) * P], Q[:, pr, b * P:(b + 1) * P],
                                                 KG[:, pr, :, :], start=True, stop=True)
                        last.then_inc(s_ready, 1)

                    def out_chunk(i, duo, c):
                        if c == 0:
                            if duo == 0:
                                pe.wait_ge(v_done, 4 * (i + 1))
                            pe.wait_ge(exp_done, E_JOBS * i + 10 * (duo + 1))
                            if not (isinstance(i, int) and i == 0 and duo == 0):
                                pe.wait_ge(ol_done, DUOS * i + duo)
                        if c == KB and not (isinstance(i, int) and i == 0 and duo == 0):
                            pe.wait_ge(og_done, DUOS * i + duo)
                        for s in range(2):
                            pr = 2 * duo + s
                            rows = slice(64 * s, 64 * (s + 1))
                            if c < KB:
                                lo, hi = max(0, 64 * c - 64), min(T, 64 * c + P)
                                at = (c % 2) * 192 + (64 if c == 0 else 0)
                                last = pe.matmul(psO[rows, 0, lo:hi], V[:, c, pr, :], pl[:, pr % 4, c // 2, at:at + hi - lo],
                                                 start=(c == 0), stop=(c == KB - 1), skip_group_check=True)
                            else:
                                last = pe.matmul(psO[rows, 1, :], V[:, 0, pr, :], pg[:, pr % 4, :], start=True, stop=True)
                        if c == KB - 1:
                            last.then_inc(ol_ready, 1)
                        if c == KB:
                            last.then_inc(og_ready, 1)

                    def score_tile(i, n):
                        pr, j = divmod(n, KB // 2 + 1)
                        if n % (E_JOBS // 2) == 0:
                            pe.wait_ge(m_in, 64 * i + 32 * (n // (E_JOBS // 2) + 1))
                        if not (isinstance(i, int) and i == 0 and n < 2):
                            pe.wait_ge(exp_done, E_JOBS * i + n - 1)
                        out = psS[:, n % 2, :]
                        if j < KB // 2:
                            for s in range(2):
                                kb = 2 * j + s
                                lo, hi = max(0, 64 * kb - 64), min(T, 64 * kb + P)
                                at = s * 192 + (64 if kb == 0 else 0)
                                pe.matmul(out[:, at:at + hi - lo], K[:, pr, kb, :, :], Q[:, pr, lo:hi],
                                          start=(s == 0), stop=False, skip_group_check=True)
                            parts = out[:, 0:384].rearrange("p (s l c) -> p s l c", s=2, c=64)[:, :, 0:3:2, :]
                            if j == 0:
                                pe.matmul(parts[:, 0, 1, :], identb[:, :], mask_k[:, 0, 1, :], start=False, stop=False,
                                          skip_group_check=True)
                                last = pe.matmul(parts[:, 1, :, :], identb[:, :], mask_k[:, 1, :, :], start=False, stop=True,
                                                 skip_group_check=True)
                            elif j == KB // 2 - 1:
                                pe.matmul(parts[:, 0, :, :], identb[:, :], mask_k[:, 0, :, :], start=False, stop=False,
                                          skip_group_check=True)
                                last = pe.matmul(parts[:, 1, 0, :], identb[:, :], mask_k[:, 1, 0, :], start=False, stop=True,
                                                 skip_group_check=True)
                            else:
                                last = pe.matmul(parts, identb[:, :], mask_k[:, :, :, :], start=False, stop=True,
                                                 skip_group_check=True)
                        else:
                            last = pe.matmul(out, KG[:, pr, :, :], Q[:, pr, :], start=True, stop=True)
                        last.then_inc(st_ready, 1)

                    def turn(i, prev, cur, nxt):
                        def take(b, signal, per, k, rel):
                            bank.take(pe, b, i, signal, per, k, rel)

                        for stage, arg in order(prev, cur, nxt):
                            if stage == "m_rows":
                                pe.wait_ge(max_done, M_JOBS * i + M_JOBS // 2 * (arg + 1))
                                take(arg, m_lo_done, 2, arg + 1, 0)
                                for q in range(QB):
                                    last = pe.transpose(psX[0:H, arg, q * P:(q + 1) * P],
                                                        negm[:, q, arg, :, :].rearrange("p k h -> p (k h)"), ident[:, :])
                                last.then_inc(m_t_ready, 1)
                            if stage == "attn_t":
                                pe.wait_ge(attn_done, QB * i)
                                for k in (1, 0):
                                    take(k, attn_t_done, KT, KT - k, -1)
                                    for q in range(QB):
                                        last = pe.transpose(psX[:, k, q * P:(q + 1) * P], attn[:, q, k * P:(k + 1) * P], ident[:, :])
                                    last.then_inc(attn_t_ready, 1)
                            if stage == "values":
                                wv = wv_sb[:, :, :].rearrange("p k (h a d) -> p k a h d", a=2, d=HD)
                                take(1 - arg, v_done, 4, 2 * (arg + 1), 0)
                                for kb in range(4 * arg, 4 * arg + 4):
                                    for k in range(KT):
                                        for a in range(2):
                                            last = pe.matmul(psX[64 * a:64 * (a + 1), 1 - arg, (kb % 4) * P:(kb % 4 + 1) * P],
                                                             xn_t[:, k, kb * 64:(kb + 1) * 64], wv[:, k, a, :, :],
                                                             start=(k == 0), stop=(k == KT - 1))
                                last.then_inc(v_ready, 1)
                            if stage == "project":
                                pe.wait_ge(attn_t_done, KT * i)
                                take(1 - arg, h1_done, 2, arg + 1, -1)
                                for q in (2 * arg, 2 * arg + 1):
                                    for k in range(KT):
                                        last = pe.matmul(psX[:, 1 - arg, (q % 2) * D:(q % 2 + 1) * D], attn_t[:, k, q * P:(q + 1) * P],
                                                         wout_sb[:, k, :], start=(k == 0), stop=(k == KT - 1))
                                last.then_inc(wout_ready, 1)
                            if stage == "embed":
                                pe.wait_ge(rows_in, 2 * QB * 16 * (i + 2))
                                take(1, la_t_done, 1, 1, 1)
                                for q in range(QB):
                                    last = pe.transpose(psX[0:R, 1, q * P:(q + 1) * P], la[:, q, :], ident[:, :])
                                last.then_inc(la_t_ready, 1)
                                pe.wait_ge(la_t_done, i + 2)
                                for j in range(2):
                                    take(j, h_done, 2, j + 1, 1)
                                    for q in (2 * j, 2 * j + 1):
                                        last = pe.matmul(psX[:, j, (q % 2) * D:(q % 2 + 1) * D], la_t[:, q * P:(q + 1) * P],
                                                         lb_t[:, :], start=True, stop=True)
                                    last.then_inc(lora_ready, 1)
                            if stage == "xn_t":
                                pe.wait_ge(xn_done, QB * (i + 2))
                                for k in range(KT):
                                    take(k, xn_t_done, KT, k + 1, 1)
                                    for q in range(QB):
                                        last = pe.transpose(psX[:, k, q * P:(q + 1) * P], xn[:, q, k * P:(k + 1) * P], ident[:, :])
                                    last.then_inc(xn_t_ready, 1)
                            if stage == "x2_t":
                                pe.wait_ge(x2_done, QB * i)
                                for k in range(KT):
                                    take(k, x2_t_done, KT, k + 1, -1)
                                    for q in range(QB):
                                        last = pe.transpose(psX[:, k, q * P:(q + 1) * P], x2[:, q, k * P:(k + 1) * P], ident[:, :])
                                    last.then_inc(x2_t_ready, 1)
                            if stage == "qk":
                                if arg == 0:
                                    pe.wait_ge(xn_t_done, KT * (i + 2))
                                take(arg % 2, qk_lo_done, 4, arg + 1, 1)
                                for k in range(KT):
                                    last = pe.matmul(psX[:, arg % 2, :], wqk[:, k, arg, :], xn_t[:, k, :],
                                                     start=(k == 0), stop=(k == KT - 1))
                                last.then_inc(qk_ready, 1)
                            if stage == "router":
                                pe.wait_ge(x2_t_done, KT * i)
                                take(1, logit_done, 1, 1, -1)
                                for q in range(QB):
                                    for k in range(KT):
                                        last = pe.matmul(psX[:, 1, q * E:(q + 1) * E], x2_t[:, k, q * P:(q + 1) * P], rw_t[:, k, :],
                                                         start=(k == 0), stop=(k == KT - 1))
                                last.then_inc(logit_ready, 1)
                            if stage == "ahead":
                                pe.wait_ge(chosen_done, i)
                                take(0, ahead_done, 1, 1, -1)
                                for q in range(QB):
                                    pe.matmul(psX[:, 0, q * E:(q + 1) * E], upper[:, :], chosen[:, q, :], start=True, stop=False)
                                    last = pe.matmul(psX[:, 0, q * E:(q + 1) * E], onesb[:, :], before[:, q, :], start=False, stop=True)
                                last.then_inc(ahead_ready, 1)
                            if stage == "exp":
                                score_tile(i, arg)
                            if stage == "out":
                                out_chunk(i, *arg)
                            if stage == "max":
                                max_tile(i + arg[0], arg[1])
                            if stage == "mix":
                                if arg == 0:
                                    pe.wait_ge(ol_done, DUOS * (i + 1))
                                    pe.wait_ge(og_done, DUOS * (i + 1))
                                for kind in range(2):
                                    take(kind, o_read, QB, arg + 1, 0)
                                    for duo in range(DUOS):
                                        last = pe.transpose(psX[:, kind, duo * P:(duo + 1) * P],
                                                            o_t[:, kind, duo, arg * P:(arg + 1) * P], ident[:, :])
                                last.then_inc(o_ready, 1)
                        bank.next_turn()
                    turns(pe, turn)

                @block.scalar
                def _(act):
                    def turn(i, prev, cur, nxt):
                        for stage, arg in order(prev, cur, nxt):
                            if stage == "m_rows":
                                act.wait_ge(m_t_ready, 2 * i + arg + 1)
                                if prev or arg:
                                    act.wait_ge(m_out, 16 * (2 * i + arg))
                                    act.wait_ge(m_lo_done, 2 * i + arg)
                                act.activation(m_hl[:, 0, :], psX[0:H, arg, :], ACT.Copy).then_inc(m_hi_done, 1)
                            if stage == "attn_t":
                                act.wait_ge(wout_ready, 2 * (i - 1))
                                for k in (1, 0):
                                    act.wait_ge(attn_t_ready, KT * (i - 1) + KT - k)
                                    act.activation(attn_t[:, k, :], psX[:, k, :], ACT.Copy).then_inc(attn_t_done, 1)
                            if stage == "embed":
                                act.wait_ge(la_t_ready, i + 2)
                                if cur:
                                    act.wait_ge(lora_ready, 2 * (i + 1))
                                act.activation(la_t[:, :], psX[0:R, 1, :], ACT.Copy).then_inc(la_t_done, 1)
                            if stage == "norm2":
                                act.wait_ge(mv2_done, i)
                                act.activation(std2[:, :], mv2[:, :, 1], ACT.Sqrt, bias=eps_b[:, :]).then_inc(std2_done, 1)
                            if stage == "norm1":
                                act.wait_ge(mv1_done, i + 2)
                                act.activation(std1[:, :], mv1[:, :, 1], ACT.Sqrt, bias=eps_b[:, :]).then_inc(std1_done, 1)
                            if stage == "xn_t":
                                for k in range(KT):
                                    act.wait_ge(xn_t_ready, KT * (i + 1) + k + 1)
                                    if k == 0 and cur:
                                        act.wait_ge(v_ready, 2 * (i + 1))
                                    act.activation(xn_t[:, k, :], psX[:, k, :], ACT.Copy).then_inc(xn_t_done, 1)
                            if stage == "x2_t":
                                for k in range(KT):
                                    act.wait_ge(x2_t_ready, KT * (i - 1) + k + 1)
                                    if k == 0:
                                        act.wait_ge(logit_ready, i - 1)
                                    act.activation(x2_t[:, k, :], psX[:, k, :], ACT.Copy).then_inc(x2_t_done, 1)
                            if stage == "qk":
                                act.wait_ge(qk_ready, 4 * (i + 1) + arg + 1)
                                if arg == 0 and cur:
                                    act.wait_ge(qk_out, 32 * (i + 1))
                                    act.wait_ge(qk_lo_done, 4 * (i + 1))
                                act.activation(qk_hi[:, arg, :], psX[:, arg % 2, :], ACT.Identity,
                                               bias=bqk[:, arg:arg + 1]).then_inc(qk_hi_done, 1)
                            if stage == "gate":
                                act.wait_ge(gate_ready, i + 2)
                                act.activation(egate[:, :], zgate[:, :], ACT.Exp, bias=neg_bg[:, :],
                                               scale=-1.0).then_inc(egate_done, 1)
                            if stage == "weights":
                                act.wait_ge(gap_done, i)
                                act.activation(egap[:, :], gap[:, :], ACT.Exp).then_inc(egap_done, 1)
                            if stage == "exp":
                                pr, j = divmod(arg, KB // 2 + 1)
                                act.wait_ge(st_ready, E_JOBS * i + arg + 1)
                                if pr % 2 == 0 and j == 0 and (prev or pr >= 4):
                                    act.wait_ge(og_ready, DUOS * i + pr // 2 - 1)
                                if j == KB // 2:
                                    act.activation(pg[:, pr % 4, :], psS[:, arg % 2, :], ACT.Exp, scale=SCALE).then_inc(exp_done, 1)
                                else:
                                    lo, hi = (64 if j == 0 else 0), (320 if j == KB // 2 - 1 else 384)
                                    act.activation(pl[:, pr % 4, j, lo:hi], psS[:, arg % 2, lo:hi], ACT.Exp,
                                                   scale=SCALE).then_inc(exp_done, 1)
                            if stage == "out" and arg[1] >= KB - 1:
                                duo, kind = arg[0], arg[1] - (KB - 1)
                                ready, done = ((ol_ready, ol_done), (og_ready, og_done))[kind]
                                act.wait_ge(ready, DUOS * i + duo + 1)
                                if prev and duo == 0 and kind == 0:
                                    act.wait_ge(o_ready, QB * i)
                                act.activation(o_t[:, kind, duo, :], psO[:, kind, :], ACT.Copy).then_inc(done, 1)
                    turns(act, turn)

                @block.vector
                def _(dve):
                    def route_top(i):
                        link = Link(dve, k_top, 9, i - 1)
                        dve.wait_ge(logit_ready, i)
                        dve.tensor_copy(logit[:, :, :], psX[:, 1, 0:QB * E].rearrange("p (q e) -> p q e", e=E)).then_inc(logit_done, 1)
                        dve.wait_ge(logit_done, i)
                        dve.sem_inc(carry["dve"], 1)
                        for q in range(QB):
                            ins = dve.max(top[:, q, :], logit[:, q, :])
                        link(ins)
                        dve.tensor_tensor(gap[:, :], top[:, :, 1], top[:, :, 0], ALU.subtract).then_inc(gap_done, 1)
                        for q in range(QB):
                            ins = dve.max_index(top_i[:, q, :], top[:, q, :], logit[:, q, :])
                        link(ins)
                        link(dve.tensor_copy(top_f[:, :, :], top_i[:, :, 0:2]))
                        hot = onehot[:, :, :, :].rearrange("p q k e -> p (q k) e")
                        link(dve.tensor_tensor(hot, iota8[:, :].unsqueeze(1).to_broadcast([P, 2 * QB, E]),
                                               top_f[:, :, :].rearrange("p q k -> p (q k)").unsqueeze(2).to_broadcast([P, 2 * QB, E]),
                                               ALU.is_equal))
                        dve.wait_ge(ahead_ready, i - 1)
                        dve.tensor_tensor(chosen[:, :, :], onehot[:, :, 0, :], onehot[:, :, 1, :], ALU.add)
                        link(dve.tensor_copy(before[:, 0, :], counts[:, :]))
                        for q in range(QB):
                            link(dve.tensor_tensor(before[:, q + 1, :], before[:, q, :], chosen[:, q, :], ALU.add))
                        dve.tensor_copy(counts[:, :], before[:, QB, :]).then_inc(chosen_done, 1)
                        link.end()

                    def route_rank(i):
                        link = Link(dve, k_rank, 6, i - 1)
                        dve.wait_ge(egap_done, i)
                        link(dve.tensor_scalar(egap1[:, :], egap[:, :], 1.0, None, ALU.add))
                        link(dve.reciprocal(prob[:, :, 0], egap1[:, :]))
                        dve.tensor_tensor(prob[:, :, 1], egap[:, :], prob[:, :, 0], ALU.mult)
                        dve.wait_ge(ahead_ready, i)
                        dve.tensor_copy(ahead[:, :, :], psX[:, 0, 0:QB * E].rearrange("p (q e) -> p q e", e=E)).then_inc(ahead_done, 1)
                        dve.wait_ge(ahead_done, i)
                        link(dve.tensor_tensor(picked[:, :, :, :], onehot[:, :, :, :],
                                               ahead[:, :, :].unsqueeze(2).to_broadcast([P, QB, 2, E]), ALU.mult))
                        link(dve.tensor_reduce(rank[:, :, :], picked[:, :, :, :], AX.X, ALU.add))
                        dve.tensor_scalar(over[:, :, :], rank[:, :, :], float(CAP), FAR, ALU.is_ge, ALU.mult)
                        link(dve.scalar_tensor_tensor(slot[:, :, :], top_f[:, :, :], float(STRIDE), rank[:, :, :],
                                                      ALU.mult, ALU.add))
                        dve.wait_ge(entry_out, 2 * QB * 16 * (i - 1))
                        dve.tensor_tensor(slot_i[:, :, :], slot[:, :, :], over[:, :, :], ALU.add)
                        dve.tensor_copy(entry[:, :, :, 0], tokid[:, :].unsqueeze(2).to_broadcast([P, QB, 2]))
                        dve.tensor_copy(entry[:, :, :, 1].bitcast(F32), prob[:, :, :]).then_inc(entry_done, 1)
                        dve.wait_ge(entry_done, i)
                        link(dve.tensor_scalar(tokid[:, :], tokid[:, :], float(T), None, ALU.add))
                        link.end()

                    def mixed(i, q, link):
                        outs = psX[:, :, :].rearrange("p k (h w) -> p k h w", w=2 * HD)
                        dve.wait_ge(o_ready, QB * i + q + 1)
                        link(dve.reciprocal(rsum[:, :, :], outs[:, :, :, HD]))
                        link(dve.tensor_tensor(coef[:, :, :], rsum[:, :, :], gates[:, :, q:q + 1].to_broadcast([P, 2, H]), ALU.mult))
                        if not (isinstance(i, int) and i == 0 and q < 2):
                            dve.wait_ge(attn_done, QB * i + q - 1)
                        dve.tensor_tensor(mix[:, q % 2, :, :, :], outs[:, :, :, 0:HD],
                                          coef[:, :, :].unsqueeze(3).to_broadcast([P, 2, H, HD]), ALU.mult).then_inc(o_read, 1)

                    def max_tile(s, n):
                        pr, q = divmod(n, QB + 1)
                        half = n // (M_JOBS // 2)
                        dve.wait_ge(s_ready, M_JOBS * s + n + 1)
                        if n % (M_JOBS // 2) == 0 and not (isinstance(s, int) and s == 0):
                            dve.wait_ge(m_t_ready, 2 * s + half - 1)
                        two = slice(2 * (pr % GP), 2 * (pr % GP) + 2)
                        if q < QB:
                            lo, hi, _ = keys_of(q)
                            dve.tensor_reduce(negm[:, q, half, 0, two],
                                              psS[:, 2 + n % 2, 0:(hi - lo) * P].rearrange("p (k a c) -> p a k c", a=2, c=64),
                                              AX.XY, ALU.max, negate=True).then_inc(max_done, 1)
                        else:
                            dve.tensor_reduce(negm[:, :, half, 1, two],
                                              psS[:, 2 + n % 2, :].rearrange("p (q a c) -> p q a c", a=2, c=64),
                                              AX.X, ALU.max, negate=True).then_inc(max_done, 1)

                    def turn(i, prev, cur, nxt):
                        if prev:
                            link2 = Link(dve, k_ln2, 2, i - 1)
                        if nxt:
                            link1 = Link(dve, k_ln1, 4, i + 1)
                        if cur:
                            linkm = Link(dve, k_mix, 2 * QB, i)
                            dve.tensor_scalar(gates[:, 0, :], gate_new[:, :], -1.0, 1.0, ALU.mult, ALU.add)
                            dve.tensor_copy(gates[:, 1, :], gate_new[:, :])
                        for stage, arg in order(prev, cur, nxt):
                            if stage == "m_rows":
                                dve.wait_ge(m_hi_done, 2 * i + arg + 1)
                                if prev or arg:
                                    dve.wait_ge(m_out, 16 * (2 * i + arg))
                                dve.tensor_tensor(m_hl[:, 1, :], psX[0:H, arg, :], m_hl[:, 0, :].bitcast(F32),
                                                  ALU.subtract).then_inc(m_lo_done, 1)
                            if stage == "values":
                                dve.wait_ge(v_ready, 2 * i + arg + 1)
                                for a in range(2):
                                    rows = slice(64 * a, 64 * (a + 1))
                                    dve.tensor_tensor(V[rows, 4 * arg:4 * arg + 4, :, 32 * a:32 * a + HD],
                                                      psX[rows, 1 - arg, :].rearrange("p (k h d) -> p k h d", k=4, d=HD),
                                                      bv[rows, :, :].unsqueeze(1).to_broadcast([64, 4, PAIRS, HD]),
                                                      ALU.add).then_inc(v_done, 1)
                            if stage == "project":
                                dve.wait_ge(wout_ready, 2 * (i - 1) + arg + 1)
                                if arg == 0:
                                    dve.wait_ge(y_out, 16 * (i - 1))
                                dve.tensor_tensor(h1[:, 2 * arg:2 * arg + 2, :], psX[:, 1 - arg, :].rearrange("p (q d) -> p q d", q=2),
                                                  hb[:, 2 * arg:2 * arg + 2, :], ALU.add).then_inc(h1_done, 1)
                            if stage == "project" and arg == 1:
                                dve.wait_ge(h1_done, 2 * i)
                                for q in range(QB):
                                    ins = dve.bn_stats(stats2[:, q, :], h1[:, q, :])
                                link2(ins)
                                dve.sem_inc(carry["dve"], 1)
                                for q in range(QB):
                                    ins = dve.bn_aggr(mv2[:, q, :], stats2[:, q, :])
                                ins.then_inc(mv2_done, 1)
                            if stage == "embed":
                                for j in range(2):
                                    dve.wait_ge(lora_ready, 2 * (i + 1) + j + 1)
                                    if j == 0:
                                        dve.wait_ge(rows_in, 2 * QB * 16 * (i + 2))
                                        if cur:
                                            dve.wait_ge(hb_done, i + 1)
                                    dve.scalar_tensor_tensor(h[:, 2 * j:2 * j + 2, :], psX[:, j, :].rearrange("p (q d) -> p q d", q=2),
                                                             LORA_SCALE, emb_t[:, 2 * j:2 * j + 2, :], ALU.mult,
                                                             ALU.add).then_inc(h_done, 1)
                                dve.wait_ge(h_done, 2 * (i + 2))
                                for q in range(QB):
                                    ins = dve.bn_stats(stats1[:, q, :], h[:, q, :])
                                link1(ins)
                                dve.sem_inc(carry["dve"], 1)
                                for q in range(QB):
                                    ins = dve.bn_aggr(mv1[:, q, :], stats1[:, q, :])
                                ins.then_inc(mv1_done, 1)
                            if stage == "norm2":
                                dve.wait_ge(std2_done, i)
                                link2(dve.reciprocal(rstd2[:, :], std2[:, :]))
                                link2.end()
                                dve.wait_ge(x2_out, 16 * (i - 1))
                                dve.wait_ge(x2_t_ready, KT * (i - 1))
                                dve.wait_ge(res_done, i - 1)
                                for q in range(QB):
                                    dve.tensor_scalar(x2[:, q, :], h1[:, q, :], mv2[:, q, 0:1], rstd2[:, q:q + 1],
                                                      ALU.subtract, ALU.mult).then_inc(x2_done, 1)
                            if stage == "norm1":
                                dve.wait_ge(std1_done, i + 2)
                                link1(dve.reciprocal(rstd1[:, :], std1[:, :]))
                                if cur:
                                    dve.wait_ge(xn_t_ready, KT * (i + 1))
                                    dve.wait_ge(xn_wg_done, i + 1)
                                for q in range(QB):
                                    dve.tensor_scalar(xn[:, q, :], h[:, q, :], mv1[:, q, 0:1], rstd1[:, q:q + 1],
                                                      ALU.subtract, ALU.mult).then_inc(xn_done, 1)
                            if stage == "qk":
                                dve.wait_ge(qk_hi_done, 4 * (i + 1) + arg + 1)
                                if arg == 0 and cur:
                                    dve.wait_ge(qk_out, 32 * (i + 1))
                                dve.scalar_tensor_tensor(qk_lo[:, arg, :], psX[:, arg % 2, :], bqk[:, arg:arg + 1],
                                                         qk_hi[:, arg, :].bitcast(F32), ALU.add,
                                                         ALU.subtract).then_inc(qk_lo_done, 1)
                            if stage == "gate":
                                if cur:
                                    dve.wait_ge(egate_done, i + 1)
                                dve.wait_ge(xn_wg_done, i + 2)
                                dve.tensor_reduce(zgate[:, :], xn_wg[:, :, :], AX.X, ALU.add).then_inc(gate_ready, 1)
                                dve.wait_ge(egate_done, i + 2)
                                link1(dve.tensor_scalar(egate1[:, :], egate[:, :], 1.0, None, ALU.add))
                                link1(dve.reciprocal(gate_new[:, :], egate1[:, :]))
                                link1.end()
                            if stage == "router":
                                route_top(i)
                            if stage == "ahead":
                                route_rank(i)
                            if stage == "max":
                                max_tile(i + arg[0], arg[1])
                            if stage == "mix":
                                mixed(i, arg, linkm)
                        if cur:
                            linkm.end()
                    turns(dve, turn)

        attn_mem.close()
        with ExitStack() as mem:
            tmp = lambda name, shape, dt=F32: sb(mem, name, shape, dt)
            HT = E * HE
            CHUNKS = [(c, min(P, HT - c)) for c in range(0, HT, P)]
            tab_rows = tmp("tab_rows", [P, len(CHUNKS), P, 2], I32)
            tok_rows = tmp("tok_rows", [P, len(CHUNKS), P])
            tok_all = tmp("tok_all", [P, HT + 2], I32)
            wt_all = tmp("wt_all", [P, HT])
            w1_raw = tmp("w1_raw", [P, KT, F])
            w2_raw = tmp("w2_raw", [P, FT, D])
            w1_hi = tmp("w1_hi", [P, KT, F], F32R)
            w1_lo = tmp("w1_lo", [P, KT, F], F32R)
            w2_hi = tmp("w2_hi", [P, FT, D], F32R)
            w2_lo = tmp("w2_lo", [P, FT, D], F32R)
            tok_in = tmp("tok_in", [P, 2], I32)
            tok_first = tmp("tok_first", [P, 2], I32)
            xg_first = tmp("xg_first", [P, 2, D])
            total_f = tmp("total_f", [P, E])
            used_i = tmp("used_i", [P, E], I32)
            tok_out = tmp("tok_out", [P, 2], I32)
            xg = tmp("xg", [P, 3, 2, D])
            xg_hi = tmp("xg_hi", [P, 3, KT, 2 * P], F32R)
            xg_lo = tmp("xg_lo", [P, 3, KT, 2 * P], F32R)
            act32 = tmp("act32", [P, 4, 2, 2 * P])
            h_hi = tmp("h_hi", [P, 3, FT, 2 * P], F32R)
            h_lo = tmp("h_lo", [P, 3, FT, 2 * P], F32R)
            out_t = tmp("out_t", [P, 3, 2, D])

            table_in, tok_rows_done, tab_t_ready, tab_done = sem("table_in"), sem("tok_rows_done"), sem("tab_t_ready"), sem("tab_done")
            w1_in, w2_in = sem("w1_in"), sem("w2_in")
            w1_hi_done, w1_lo_done, w2_hi_done, w2_lo_done = sem("w1_hi_done"), sem("w1_lo_done"), sem("w2_hi_done"), sem("w2_lo_done")
            tok_in_done, tok_out_done, xg_in = sem("tok_in_done"), sem("tok_out_done"), sem("xg_in")
            tok_first_done, first_in = sem("tok_first_done"), sem("first_in")
            rows_ready, out_free = sem("rows_ready"), sem("out_free")
            used_ready, used_f_done, used_done = sem("used_ready"), sem("used_f_done"), sem("used_done")
            xg_t_ready, xg_hi_done, xg_lo_done = sem("xg_t_ready"), sem("xg_hi_done"), sem("xg_lo_done")
            up_ready, silu_done, h_lo_done = sem("up_ready"), sem("silu_done"), sem("h_lo_done")
            down_ready, out_done, y_added = sem("down_ready"), sem("out_done"), sem("y_added")

            TE = -(-HE // 2)
            LAST = HE - 2 * (TE - 1)
            TURNS = (TE - 5) // 2 + 1

            class Tile:
                def __init__(self, e, j, like):
                    last = like == TE - 1
                    self.e, self.first, self.second = e, like == 0, like == 1
                    self.after = None if last else (e, j + 1, like + 1)
                    self.buf = 2 if last and TE % 2 else like % 2
                    self.halves = LAST if last else 2
                    self.t = e * TE + j
                    self.h0 = e * HE + 2 * j
                    self.n1 = e * (TE - 1) + j
                    self.start = isinstance(self.t, int) and self.t == 0

            def tiles(eng, fetch, step, skip):
                def guarded(used, j, prev, cur, nxt):
                    with eng.If(used > 2 * P * (j - 1)):
                        step(prev, cur, nxt)
                    with eng.Else():
                        skip(prev, cur, nxt)

                def expert(e):
                    used = eng.value_load(used_i[0:1, bass.ds(e, 1)], min_val=0, max_val=HE * P)
                    fetch(Tile(e, 0, 0))
                    row = [None] + [Tile(e, j, j) for j in range(TE)] + [None]
                    looped = range(2, 2 * TURNS) if TURNS > 2 else range(0)
                    for j in range(TE + 1):
                        if j < 2:
                            step(*row[j:j + 2], row[j + 2])
                        elif j not in looped:
                            guarded(used, j, row[j], row[j + 1], row[j + 2] if j < TE else None)
                        elif j == 2:
                            with eng.Fori(1, TURNS) as m:
                                for s in range(2):
                                    guarded(used, 2 * m + s, *(Tile(e, 2 * m + s + d, 2 + s + d) for d in (-1, 0, 1)))

                expert(0)
                with eng.Fori(1, E) as e:
                    expert(e)

            with nc.Block() as block:
                @block.sync
                def _(sp):
                    for c, (first, n) in enumerate(CHUNKS):
                        sp.dma_start(tab_rows[0:n, c, :, :],
                                     table[first * P:(first + n) * P, :].rearrange("(h p) w -> h p w", p=P)).then_inc(table_in, 16)

                    def weights(e):
                        sp.dma_start(w1_raw[:, :, :], w1[e].rearrange("(k p) f -> p k f", p=P)).then_inc(w1_in, 16)
                        if not isinstance(e, int):
                            sp.wait_ge(w2_hi_done, e)
                            sp.wait_ge(w2_lo_done, e)
                        sp.dma_start(w2_raw[:, :, :], w2[e].rearrange("(f p) d -> p f d", p=P)).then_inc(w2_in, 16)
                    weights(0)
                    with sp.Fori(1, E) as e:
                        sp.wait_ge(w1_lo_done, 2 * e)
                        sp.sem_inc(carry["sp"], 1)
                        weights(e)

                @block.gpsimd
                def _(pool):
                    asked, summed = pool.alloc_register("asked"), pool.alloc_register("summed")
                    pool.reg_mov(asked, 0)
                    pool.reg_mov(summed, 0)

                    def gather(tile, tokens, rows, done, landed, count):
                        pool.tensor_copy(tokens[:, 0:tile.halves],
                                         tok_all[:, bass.ds(tile.h0, tile.halves)]).then_inc(done, 1)
                        pool.wait_ge(done, count)
                        pool.sem_inc(carry["pool"], 1)
                        for s in range(tile.halves):
                            pool.indirect_dma_start(out=rows[:, s, :], out_offset=None, in_=x2_rows[:, :],
                                                    in_offset=bass.IndirectOffsetOnAxis(ap=tokens[:, s:s + 1], axis=0),
                                                    ).then_inc(landed, 16)

                    def ahead(tile):
                        if not tile.start:
                            pool.wait_ge(xg_t_ready, tile.t)
                        pool.sem_inc(carry["pool"], 1)
                        new = Tile(*tile.after)
                        gather(new, tok_in, xg[:, new.buf], tok_in_done, xg_in, new.n1)
                        pool.reg_add(asked, asked, 16 * new.halves)
                        pool.wait_ge(xg_in, asked)
                        pool.sem_inc(rows_ready, 1)

                    def fetch(tile):
                        ahead(tile)

                    def step(prev, cur, nxt):
                        if nxt and nxt.after:
                            ahead(nxt)
                        if nxt and nxt.second:
                            gather(Tile(cur.e + 1, 0, 0), tok_first, xg_first, tok_first_done, first_in, cur.e + 2)
                        if prev:
                            if not prev.start:
                                pool.wait_ge(y_added, summed)
                            pool.sem_inc(out_free, 1)
                            pool.tensor_copy(tok_out[:, 0:prev.halves],
                                             tok_all[:, bass.ds(prev.h0, prev.halves)]).then_inc(tok_out_done, 1)
                            pool.wait_ge(tok_out_done, prev.t + 1)
                            for s in range(prev.halves):
                                if s:
                                    pool.wait_ge(y_added, summed)
                                pool.wait_ge(out_done, prev.h0 + s + 1)
                                pool.sem_inc(carry["pool"], 1)
                                pool.indirect_dma_start(out=y[:, :], in_=out_t[:, prev.buf, s, :], in_offset=None,
                                                        out_offset=bass.IndirectOffsetOnAxis(ap=tok_out[:, s:s + 1], axis=0),
                                                        compute_op=ALU.add).then_inc(y_added, 16)
                                pool.reg_add(summed, summed, 16)

                    def skip(prev, cur, nxt):
                        pool.wait_ge(y_added, summed)
                        if nxt and nxt.after:
                            pool.sem_inc(tok_in_done, 1)
                            pool.sem_inc(rows_ready, 1)
                        pool.sem_inc(tok_out_done, 1)
                        pool.sem_inc(out_free, 1)

                    pool.wait_ge(tab_done, 1)
                    pool.sem_inc(carry["pool"], 1)
                    gather(Tile(0, 0, 0), tok_first, xg_first, tok_first_done, first_in, 1)
                    pool.wait_ge(used_done, 1)
                    tiles(pool, fetch, step, skip)
                    pool.wait_ge(first_in, 32 * (E + 1))
                    pool.wait_ge(y_added, summed)

                @block.tensor
                def _(pe):
                    pe.wait_ge(tok_rows_done, 1)
                    for c, (first, n) in enumerate(CHUNKS):
                        pe.transpose(psX[:, 0, first:first + n], tok_rows[0:n, c, :], ident[0:n, 0:n])
                        last = pe.transpose(psX[:, 1, first:first + n], tab_rows[0:n, c, :, 1].bitcast(F32), ident[0:n, 0:n])
                    last.then_inc(tab_t_ready, 1)
                    pe.matmul(psO[:, 0, 0:E], onesb[:, :], counts[:, :], start=True, stop=True).then_inc(used_ready, 1)
                    pe.wait_ge(used_done, 1)

                    def transposed(tile, rows):
                        if tile.start:
                            pe.wait_ge(tab_done, 1)
                        else:
                            pe.wait_ge(xg_lo_done, tile.t)
                        for k in range(KT):
                            for s in range(tile.halves):
                                last = pe.transpose(psX[:, 0, (2 * k + s) * P:(2 * k + s + 1) * P],
                                                    rows[:, s, k * P:(k + 1) * P], ident[:, :])
                        last.then_inc(xg_t_ready, 1)

                    def fetch(tile):
                        pe.wait_ge(first_in, 32 * (tile.e + 1))
                        transposed(tile, xg_first)

                    def skip(prev, cur, nxt):
                        pe.wait_ge(down_ready, prev.h0)
                        pe.wait_ge(up_ready, 4 * (prev.t + 1))
                        if cur:
                            pe.wait_ge(xg_t_ready, prev.t + 2)
                            pe.sem_inc(up_ready, 4)
                        if nxt:
                            pe.sem_inc(xg_t_ready, 1)
                        pe.sem_inc(down_ready, prev.halves)

                    def step(prev, cur, nxt):
                        if cur:
                            cols = cur.halves * P
                            pe.wait_ge(xg_lo_done, cur.t + 1)
                            for f in range(FT):
                                if cur.first and f % 4 == 0:
                                    pe.wait_ge(w1_lo_done, 2 * cur.e + f // 4 + 1)
                                if f % 2 == 0 and not cur.start:
                                    pe.wait_ge(silu_done, 4 * cur.t + f // 2 - 3)
                                for k in range(KT):
                                    fs = slice(f * P, (f + 1) * P)
                                    for n, (w, x) in enumerate(((w1_hi, xg_hi), (w1_hi, xg_lo), (w1_lo, xg_hi))):
                                        last = pe.matmul(psS[:, f // 2, (f % 2) * 256:(f % 2) * 256 + cols], w[:, k, fs],
                                                         x[:, cur.buf, k, 0:cols], start=(k == 0 and n == 0),
                                                         stop=(k == KT - 1 and n == 2))
                                if f % 2:
                                    last.then_inc(up_ready, 1)
                        if nxt:
                            pe.wait_ge(rows_ready, nxt.n1)
                            transposed(nxt, xg[:, nxt.buf])
                        if prev:
                            pe.wait_ge(h_lo_done, 4 * (prev.t + 1))
                            if prev.first:
                                pe.wait_ge(w2_lo_done, prev.e + 1)
                            for s in range(prev.halves):
                                if not prev.start:
                                    pe.wait_ge(out_done, prev.h0)
                                for f in range(FT):
                                    ts = slice(s * P, (s + 1) * P)
                                    for n, (h_, w) in enumerate(((h_hi, w2_hi), (h_hi, w2_lo), (h_lo, w2_hi))):
                                        last = pe.matmul(psO[:, s, 0:D], h_[:, prev.buf, f, ts], w[:, f, :],
                                                         start=(f == 0 and n == 0), stop=(f == FT - 1 and n == 2))
                                last.then_inc(down_ready, 1)
                    tiles(pe, fetch, step, skip)

                @block.scalar
                def _(act):
                    def transposed(tile):
                        act.wait_ge(xg_t_ready, tile.t + 1)
                        cols = tile.halves * P
                        act.activation(xg_hi[:, tile.buf, :, 0:cols],
                                       psX[:, 0, :].rearrange("p (k c) -> p k c", k=KT)[:, :, 0:cols], ACT.Copy).then_inc(xg_hi_done, 1)

                    def fetch(tile):
                        act.wait_ge(w1_in, 16 * (tile.e + 1))
                        for g in range(2):
                            fs = slice(g * F // 2, (g + 1) * F // 2)
                            act.activation(w1_hi[:, :, fs], w1_raw[:, :, fs], ACT.Copy).then_inc(w1_hi_done, 1)
                            if g == 0:
                                transposed(tile)

                    def skip(prev, cur, nxt):
                        if cur:
                            act.wait_ge(silu_done, 4 * (prev.t + 1))
                            act.sem_inc(silu_done, 4)
                        if nxt:
                            act.wait_ge(xg_hi_done, prev.t + 2)
                            act.sem_inc(xg_hi_done, 1)

                    def step(prev, cur, nxt):
                        if cur and cur.second:
                            act.wait_ge(w2_in, 16 * (cur.e + 1))
                            if not prev.start:
                                act.wait_ge(down_ready, prev.h0)
                            act.activation(w2_hi[:, :, :], w2_raw[:, :, :], ACT.Copy).then_inc(w2_hi_done, 1)
                        if cur:
                            cols = cur.halves * P
                            for b in range(4):
                                act.wait_ge(up_ready, 4 * cur.t + b + 1)
                                if not cur.start:
                                    act.wait_ge(h_lo_done, 4 * cur.t + b - 3)
                                src = psS[:, b, :].rearrange("p (f c) -> p f c", f=2)[:, :, 0:cols]
                                act.activation(act32[:, b, :, 0:cols], src, ACT.Silu)
                                act.activation(h_hi[:, cur.buf, 2 * b:2 * b + 2, 0:cols], src, ACT.Silu).then_inc(silu_done, 1)
                        if nxt:
                            transposed(nxt)
                    act.wait_ge(used_done, 1)
                    tiles(act, fetch, step, skip)

                @block.vector
                def _(dve):
                    dve.wait_ge(table_in, 16 * len(CHUNKS))
                    for c, (first, n) in enumerate(CHUNKS):
                        ins = dve.tensor_copy(tok_rows[0:n, c, :], tab_rows[0:n, c, :, 0])
                    ins.then_inc(tok_rows_done, 1)
                    dve.wait_ge(tab_t_ready, 1)
                    dve.tensor_copy(tok_all[:, 0:HT], psX[:, 0, 0:HT])
                    dve.tensor_copy(tok_all[:, HT:HT + 2], psX[:, 0, 0:2])
                    dve.tensor_copy(wt_all[:, :], psX[:, 1, 0:HT]).then_inc(tab_done, 1)

                    def transposed(tile):
                        dve.wait_ge(xg_hi_done, tile.t + 1)
                        cols = tile.halves * P
                        dve.tensor_tensor(xg_lo[:, tile.buf, :, 0:cols],
                                          psX[:, 0, :].rearrange("p (k c) -> p k c", k=KT)[:, :, 0:cols],
                                          xg_hi[:, tile.buf, :, 0:cols].bitcast(F32), ALU.subtract).then_inc(xg_lo_done, 1)

                    def fetch(tile):
                        for g in range(2):
                            fs = slice(g * F // 2, (g + 1) * F // 2)
                            dve.wait_ge(w1_hi_done, 2 * tile.e + g + 1)
                            dve.tensor_tensor(w1_lo[:, :, fs], w1_raw[:, :, fs], w1_hi[:, :, fs].bitcast(F32),
                                              ALU.subtract).then_inc(w1_lo_done, 1)
                            if g == 0:
                                transposed(tile)

                    def skip(prev, cur, nxt):
                        if cur:
                            dve.wait_ge(h_lo_done, 4 * (prev.t + 1))
                            dve.sem_inc(h_lo_done, 4)
                        if nxt:
                            dve.wait_ge(xg_lo_done, prev.t + 2)
                            dve.sem_inc(xg_lo_done, 1)
                        dve.wait_ge(out_done, prev.h0)
                        dve.sem_inc(out_done, prev.halves)

                    def step(prev, cur, nxt):
                        if cur and cur.second:
                            dve.wait_ge(w2_hi_done, cur.e + 1)
                            dve.tensor_tensor(w2_lo[:, :, :], w2_raw[:, :, :], w2_hi[:, :, :].bitcast(F32),
                                              ALU.subtract).then_inc(w2_lo_done, 1)
                        if cur:
                            cols = cur.halves * P
                            for b in range(4):
                                dve.wait_ge(silu_done, 4 * cur.t + b + 1)
                                dve.tensor_tensor(h_lo[:, cur.buf, 2 * b:2 * b + 2, 0:cols], act32[:, b, :, 0:cols],
                                                  h_hi[:, cur.buf, 2 * b:2 * b + 2, 0:cols].bitcast(F32),
                                                  ALU.subtract).then_inc(h_lo_done, 1)
                        if nxt:
                            transposed(nxt)
                        if prev:
                            for s in range(prev.halves):
                                dve.wait_ge(down_ready, prev.h0 + s + 1)
                                if s == 0 and not prev.start:
                                    dve.wait_ge(out_free, prev.t)
                                dve.tensor_scalar(out_t[:, prev.buf, s, :], psO[:, s, 0:D],
                                                  wt_all[:, bass.ds(prev.h0 + s, 1)], None, ALU.mult).then_inc(out_done, 1)
                    dve.wait_ge(used_ready, 1)
                    dve.tensor_copy(total_f[:, :], psO[:, 0, 0:E]).then_inc(used_f_done, 1)
                    dve.wait_ge(used_f_done, 1)
                    dve.tensor_scalar(used_i[:, :], total_f[:, :], float(HE * P), None, ALU.min).then_inc(used_done, 1)
                    dve.wait_ge(used_done, 1)
                    tiles(dve, fetch, step, skip)


_INS = ["x", "L0_tok_emb_weight", "L0_tok_lora_A", "L0_tok_lora_B", "L0_attn_Wqkv", "L0_attn_bqkv", "L0_attn_Wout",
        "L0_attn_bout", "L0_attn_Wg", "L0_attn_bg", "L0_ffn_router_w", "L0_ffn_w1", "L0_ffn_w2"]


def kernel(**inputs):
    import numpy as _np
    import concourse.bacc as _bacc
    from concourse import mybir as _mybir
    from concourse.bass_utils import run_bass_kernel_spmd as _run

    nc = _bacc.Bacc("TRN2", target_bir_lowering=False, num_devices=1)
    arrays, args = {}, []
    for name in _INS:
        a = _np.ascontiguousarray(inputs[name])
        arrays[f"in_{name}"] = a
        args.append(nc.dram_tensor(f"in_{name}", a.shape, _mybir.dt.from_np(a.dtype), kind="ExternalInput").ap())
    seqs = inputs["x"].shape[0]
    args.append(nc.dram_tensor("out_y", [seqs * T + P, D], _mybir.dt.float32, kind="ExternalOutput").ap())
    build(nc, *args)
    r = _run(nc, [arrays], core_ids=[0])
    return r.results[0]["out_y"][:seqs * T].reshape(seqs, T, D)
```
